# Optimizing a Trainium2 kernel written in Bass

```python
import numpy as np
import jax
import jax.numpy as jnp

def _softmax(x, axis=-1):
    return jax.nn.softmax(x, axis=axis)

def _gelu(x):
    return jax.nn.gelu(x, approximate=True)

def _silu(x):
    return jax.nn.silu(x)

def _sigmoid(x):
    return jax.nn.sigmoid(x)

def _layernorm(x, axis=-1, eps=1e-05):
    m = jnp.mean(x, axis=axis, keepdims=True)
    v = jnp.var(x, axis=axis, keepdims=True)
    return (x - m) / jnp.sqrt(v + eps)

def _scatter_add(tgt, idx, src, axis=0):
    return tgt.at[idx].add(src)

def _segment_sum(src, seg, n):
    return jax.ops.segment_sum(src, seg, n)
kernel_name = 'mk_gnn_resnorm_d4_gnn_r32_6ad6e3'

def setup_inputs(seed: int=0):
    np.random.seed(seed)
    _w = jnp.asarray

    def _rec_inputs():
        import jax
        import jax.numpy as jnp
        _gk = jax.random.key(seed)
        x = -0.000202 + 1 * jax.random.normal(jax.random.fold_in(_gk, 1), (3125, 128), jnp.float32)
        src = jax.random.randint(jax.random.fold_in(_gk, 2), (100000,), 0, 3125, jnp.int32)
        dst = jax.random.randint(jax.random.fold_in(_gk, 3), (100000,), 0, 3125, jnp.int32)
        _o = jnp.argsort(dst, stable=True)
        src = src[_o]
        dst = dst[_o]
        edge_attr_32 = -5.25733e-05 + 1.00007 * jax.random.normal(jax.random.fold_in(_gk, 12), (100000, 32), jnp.float32)
        edge_type_8 = jax.random.randint(jax.random.fold_in(_gk, 14), (100000,), 0, 8, jnp.int32)
        return (x, src, dst, edge_attr_32, edge_type_8)
    x, src, dst, edge_attr_32, edge_type_8 = _rec_inputs()

    def _L0_gnn_setup():
        import jax, jax.numpy as jnp
        import numpy as np
        IN_DIM = 128
        OUT_DIM = 128
        NUM_RELS = 8
        N_NODES = 50000
        N_EDGES = 15625
        key = jax.random.key(seed)
        k_x, k_ei_s, k_ei_d, k_et, k_w, k_sw = jax.random.split(key, 6)
        x = jax.random.normal(k_x, (N_NODES, IN_DIM), dtype=jnp.float32)
        src = jax.random.randint(k_ei_s, (N_EDGES,), 0, N_NODES)
        dst = jax.random.randint(k_ei_d, (N_EDGES,), 0, N_NODES)
        edge_index = jnp.stack([src, dst], axis=0).astype(jnp.int64)
        edge_type = jax.random.randint(k_et, (N_EDGES,), 0, NUM_RELS).astype(jnp.int64)
        bw = float(np.sqrt(6.0 / (IN_DIM + OUT_DIM)))
        weight = jax.random.uniform(k_w, (NUM_RELS, IN_DIM, OUT_DIM), dtype=jnp.float32, minval=-bw, maxval=bw)
        self_loop_weight = jax.random.uniform(k_sw, (IN_DIM, OUT_DIM), dtype=jnp.float32, minval=-bw, maxval=bw)
        bias = jnp.zeros((OUT_DIM,), dtype=jnp.float32)
        return {'x': x, 'weight': weight, 'self_loop_weight': self_loop_weight, 'bias': bias, 'edge_index': edge_index, 'edge_type': edge_type, 'num_entities': N_NODES}
    _L0_gnn_all = _L0_gnn_setup()
    _L0_gnn_in = {k: v for k, v in _L0_gnn_all.items() if k in ('weight', 'self_loop_weight', 'bias')}
    del _L0_gnn_all

    def _L1_gnn_setup():
        import jax, jax.numpy as jnp
        import numpy as np
        N_NODES = 50000
        N_EDGES = 15625
        G_DIM = 128
        R_DIM = 32
        INTER_DIM = 8 * int(np.ceil((G_DIM + R_DIM) / 16))
        OUT_DIM = 128
        SLOPE = 0.01

        def _xavier_normal(key, shape, gain):
            fan_out, fan_in = shape
            std = gain * np.sqrt(2.0 / (fan_in + fan_out))
            return jax.random.normal(key, shape, dtype=jnp.float32) * std
        key = jax.random.key(seed)
        k1, k2, k3, k4, k5, k6 = jax.random.split(key, 6)
        gain = float(np.sqrt(2.0 / (1.0 + SLOPE ** 2)))
        return {'input_gate_embedding': jax.random.normal(k1, (N_NODES, G_DIM), dtype=jnp.float32), 'edge_reg_embedding': jax.random.normal(k2, (N_EDGES, R_DIM), dtype=jnp.float32), 'src': jax.random.randint(k3, (N_EDGES,), 0, N_NODES, dtype=jnp.int32), 'dst': jax.random.randint(k4, (N_EDGES,), 0, N_NODES, dtype=jnp.int32), 'W1': _xavier_normal(k5, (INTER_DIM, G_DIM + R_DIM), gain), 'W2': _xavier_normal(k6, (OUT_DIM, G_DIM + INTER_DIM), gain), 'b2': jnp.zeros((OUT_DIM,), dtype=jnp.float32)}
    _L1_gnn_all = _L1_gnn_setup()
    _L1_gnn_in = {k: v for k, v in _L1_gnn_all.items() if k in ('W1', 'W2', 'b2')}
    del _L1_gnn_all

    def _L2_gnn_setup():
        import jax, jax.numpy as jnp
        import numpy as np
        N_NODES = 50000
        N_EDGES = 25000
        IN_F = 128
        HEADS = 4
        OUT_F = 32
        NEG_SLOPE = 0.2
        EPS = 1e-09
        key = jax.random.key(seed)
        k1, k2, k3, k4, k5 = jax.random.split(key, 5)
        x = jax.random.normal(k1, (N_NODES, IN_F), dtype=jnp.float32)
        edge_index = jax.random.randint(k2, (2, N_EDGES), 0, N_NODES, dtype=jnp.int64)
        W = jax.random.normal(k3, (HEADS * OUT_F, IN_F), dtype=jnp.float32) * 0.05
        att = jax.random.normal(k4, (HEADS, 2 * OUT_F), dtype=jnp.float32) * 0.05
        bias = jax.random.normal(k5, (HEADS * OUT_F,), dtype=jnp.float32) * 0.05
        return {'x': x, 'edge_index': edge_index, 'W': W, 'att': att, 'bias': bias}
    _L2_gnn_all = _L2_gnn_setup()
    _L2_gnn_in = {k: v for k, v in _L2_gnn_all.items() if k in ('W', 'att', 'bias')}
    del _L2_gnn_all

    def _L3_gnn_setup():
        import jax, jax.numpy as jnp
        import numpy as np
        N_NODES = 50000
        N_EDGES = 50000
        IN_FEAT = 128
        OUT_FEAT = 128
        EPS = 1e-12
        key = jax.random.key(seed)
        k1, k2, k3, k4 = jax.random.split(key, 4)
        x = jax.random.normal(k1, (N_NODES, IN_FEAT), dtype=jnp.float32)
        edge_index = jax.random.randint(k2, (2, N_EDGES), 0, N_NODES, dtype=jnp.int64)
        scale = 1.0 / np.sqrt(2 * IN_FEAT)
        W = jax.random.uniform(k3, (2 * IN_FEAT, OUT_FEAT), dtype=jnp.float32, minval=-scale, maxval=scale)
        b = jax.random.uniform(k4, (OUT_FEAT,), dtype=jnp.float32, minval=-scale, maxval=scale)
        return {'x': x, 'edge_index': edge_index, 'W': W, 'b': b}
    _L3_gnn_all = _L3_gnn_setup()
    _L3_gnn_in = {k: v for k, v in _L3_gnn_all.items() if k in ('W', 'b')}
    del _L3_gnn_all
    return {'x': x, 'src': src, 'dst': dst, 'edge_attr_32': edge_attr_32, 'edge_type_8': edge_type_8, 'L0_gnn_weight': _L0_gnn_in['weight'], 'L0_gnn_self_loop_weight': _L0_gnn_in['self_loop_weight'], 'L0_gnn_bias': _L0_gnn_in['bias'], 'L1_gnn_W1': _L1_gnn_in['W1'], 'L1_gnn_W2': _L1_gnn_in['W2'], 'L1_gnn_b2': _L1_gnn_in['b2'], 'L2_gnn_W': _L2_gnn_in['W'], 'L2_gnn_att': _L2_gnn_in['att'], 'L2_gnn_bias': _L2_gnn_in['bias'], 'L3_gnn_W': _L3_gnn_in['W'], 'L3_gnn_b': _L3_gnn_in['b']}

def reference(x, src, dst, edge_attr_32, edge_type_8, L0_gnn_weight, L0_gnn_self_loop_weight, L0_gnn_bias, L1_gnn_W1, L1_gnn_W2, L1_gnn_b2, L2_gnn_W, L2_gnn_att, L2_gnn_bias, L3_gnn_W, L3_gnn_b):
    import jax
    import jax.numpy as jnp

    def _L0_gnn_ref(x, weight, self_loop_weight, bias, edge_index, edge_type, num_entities):
        import jax, jax.numpy as jnp
        import numpy as np
        IN_DIM = 128
        OUT_DIM = 128
        NUM_RELS = 8
        N_NODES = 50000
        N_EDGES = 15625
        hr = jnp.einsum('nd,rdo->rno', x, weight)
        src, dst = (edge_index[0], edge_index[1])
        msg = hr[edge_type, src]
        agg = jax.ops.segment_sum(msg, dst, num_segments=num_entities)
        out = agg + x @ self_loop_weight + bias
        return jax.nn.relu(out)

    def _L1_gnn_ref(input_gate_embedding, edge_reg_embedding, src, dst, W1, W2, b2):
        import jax, jax.numpy as jnp
        import numpy as np
        N_NODES = 50000
        N_EDGES = 15625
        G_DIM = 128
        R_DIM = 32
        INTER_DIM = 8 * int(np.ceil((G_DIM + R_DIM) / 16))
        OUT_DIM = 128
        SLOPE = 0.01

        def _xavier_normal(key, shape, gain):
            fan_out, fan_in = shape
            std = gain * np.sqrt(2.0 / (fan_in + fan_out))
            return jax.random.normal(key, shape, dtype=jnp.float32) * std
        n_nodes = input_gate_embedding.shape[0]
        msg = jnp.concatenate([input_gate_embedding[src], edge_reg_embedding], axis=1)
        h = jax.nn.leaky_relu(msg @ W1.T, negative_slope=SLOPE)
        summed = jax.ops.segment_sum(h, dst, num_segments=n_nodes)
        deg = jax.ops.segment_sum(jnp.ones((dst.shape[0],), dtype=h.dtype), dst, num_segments=n_nodes)
        mean_nbr = summed / jnp.maximum(deg, 1.0)[:, None]
        concat = jnp.concatenate([input_gate_embedding, mean_nbr], axis=1)
        return jax.nn.leaky_relu(concat @ W2.T + b2, negative_slope=SLOPE)

    def _L2_gnn_ref(x, edge_index, W, att, bias):
        import jax, jax.numpy as jnp
        import numpy as np
        N_NODES = 50000
        N_EDGES = 25000
        IN_F = 128
        HEADS = 4
        OUT_F = 32
        NEG_SLOPE = 0.2
        EPS = 1e-09
        N = x.shape[0]
        H = att.shape[0]
        D = att.shape[1] // 2
        h = (x @ W.T).reshape(N, H, D)
        loops = jnp.arange(N, dtype=edge_index.dtype)
        src = jnp.concatenate([edge_index[0], loops])
        dst = jnp.concatenate([edge_index[1], loops])
        hl = jax.nn.leaky_relu(h, negative_slope=NEG_SLOPE)
        s_src = jnp.einsum('nhd,hd->nh', hl, att[:, :D])
        s_dst = jnp.einsum('nhd,hd->nh', hl, att[:, D:])
        scores = s_src[src] + s_dst[dst]
        e = jnp.exp(scores)
        denom = jax.ops.segment_sum(e, dst, num_segments=N)
        w = e / (denom[dst] + EPS)
        msg = h[src] * w[:, :, None]
        out = jax.ops.segment_sum(msg, dst, num_segments=N)
        return out.reshape(N, H * D) + bias

    def _L3_gnn_ref(x, edge_index, W, b):
        import jax, jax.numpy as jnp
        import numpy as np
        N_NODES = 50000
        N_EDGES = 50000
        IN_FEAT = 128
        OUT_FEAT = 128
        EPS = 1e-12
        gathered = x[edge_index[0]]
        agg = jax.ops.segment_sum(gathered, edge_index[1], num_segments=x.shape[0])
        h = jnp.concatenate([x, agg], axis=1)
        proj = jax.nn.relu(h @ W + b)
        norm = jnp.maximum(jnp.linalg.norm(proj, axis=-1, keepdims=True), EPS)
        return proj / norm
    edge_index = jnp.stack([src, dst])
    x = _layernorm(x + _L0_gnn_ref(x, L0_gnn_weight, L0_gnn_self_loop_weight, L0_gnn_bias, edge_index, edge_type_8, 3125), axis=-1)
    x = _layernorm(x + _L1_gnn_ref(x, edge_attr_32, src, dst, L1_gnn_W1, L1_gnn_W2, L1_gnn_b2), axis=-1)
    x = _layernorm(x + _L2_gnn_ref(x, edge_index, L2_gnn_W, L2_gnn_att, L2_gnn_bias), axis=-1)
    x = _layernorm(x + _L3_gnn_ref(x, edge_index, L3_gnn_W, L3_gnn_b), axis=-1)
    return x

_drawn_inputs = setup_inputs


def setup_inputs(seed=0):
    import zlib

    import numpy as np

    out = dict(_drawn_inputs(seed))
    spreads = {'L0_gnn_bias': (0.0, 0.302), 'L1_gnn_b2': (0.0, 0.1)}
    factors = {'L2_gnn_att': 3.993, 'L3_gnn_b': 64.0}
    for name, (base, spread) in spreads.items():
        noise = np.random.default_rng([zlib.crc32(name.encode()), seed]).standard_normal(out[name].shape)
        drawn = base * np.exp(spread * noise) if base else spread * noise
        out[name] = jnp.asarray(drawn.astype(out[name].dtype))
    for name, factor in factors.items():
        out[name] = (out[name] * factor).astype(out[name].dtype)
    return out
```

```python
import concourse.bass as bass
from concourse import mybir
from contextlib import ExitStack

F32 = mybir.dt.float32
I32 = mybir.dt.int32
BF16 = mybir.dt.bfloat16
F16 = mybir.dt.float16
U8 = mybir.dt.uint8
ALU = mybir.AluOpType
ACT = mybir.ActivationFunctionType
X = mybir.AxisListType.X

P = 128
N = 3125
F = 128
E = 100000
RELS = 8
R = 32
HID = 80
HEADS, HD = 4, 32
WIN = 125
NW = N // WIN
CH = 5
NC = NW // CH
T = 4
GE = P * T
NG = -(-E // GE)
SLOTS = 4
NI = NG // SLOTS
VW = 25
SB = N // VW
NPAD = N + VW
VISITS = N // VW + 1
KEYS = VW * VW
FAR = 1024
PACK = 4096
AB = 1608
HOTS = 2 * T + 1
SETS = 3
XHOTS = [T + 1, 1]
HG = NG // 2
LASTE = E - (NG - 1) * GE
ACCW = 136
TABW = [F, HID, F + HEADS, F]
SUMW = [F, HID + 1, F + HEADS, F]
EPS = 1e-5
FREED = (1, 2, 4, 5, 3)
POOLS = (4,)
ACTS = (0, 1, 2, 3)
STEPS = [2, 11, 39, 23, 15]
ADDS_AFTER = {3: (3, 8, 16, 19, 23), 4: (2, 6, 9, 14, 15)}


def resgnn(nc, x_in, src, dst, ea, etype, W0, Wself, b0, W1, W2, b2, Wg, att, bg, W3, b3, out):
    ctx = ExitStack()
    with ctx:
        def sb(name, shape, dt=F32):
            return ctx.enter_context(nc.sbuf_tensor(name, shape, dt))

        def ps(name, shape):
            return ctx.enter_context(nc.psum_tensor(name, shape, F32))

        def sem(name):
            return ctx.enter_context(nc.semaphore(name))

        def sems(name, which):
            return {n: sem(f"{name}_{n}") for n in which}

        def carve(buf, parts, at, cols, dt):
            size = cols * (4 if dt in (F32, I32) else 2)
            return buf[0:parts, at:at + size].bitcast(dt)

        ident = sb("ident", [P, P])
        iota = sb("iota", [P, WIN])
        iota16 = sb("iota16", [P, KEYS + 1], F16)
        kcode = sb("kcode", [P, VISITS])
        kloc = sb("kloc", [P, VISITS])
        ones = sb("ones", [P, P])
        wstart = sb("wstart", [P, NW])
        counts = sb("counts", [P, NI * AB], U8)
        cnt = counts[0:SB, 0:VW * NPAD].rearrange("p (h d) -> p h d", h=VW)
        table0 = carve(counts, WIN, 0, CH * RELS * F, F32).rearrange("p (s n) -> p s n", s=CH)
        at = CH * RELS * F * 4
        w0 = carve(counts, P, at, RELS * F, F32).rearrange("p (r f) -> p r f", r=RELS)
        at += RELS * F * 4
        LATE = at
        stage = carve(counts, HG, at, 6 * GE, I32).rearrange("p (a h e) -> p a h e", a=3, h=2)
        at += 6 * GE * 4
        staged = carve(counts, HG, at, 6 * GE, F32).rearrange("p (a h e) -> p a h e", a=3, h=2)
        at += 6 * GE * 4
        w1raw = carve(counts, HID, at, F + R, F32)
        w1rep = carve(counts, HID, at + 1024, T * R, F32).rearrange("p (k r) -> p k r", k=T)
        w2raw = carve(counts, P, at + 2048, F + HID, F32)
        wgraw = carve(counts, P, at + 3072, F, F32)
        at += 4096
        setf = [carve(counts, P, at + n * NG * T * 4, NG * T, F32).rearrange("p (g k) -> p g k", k=T)
                for n in range(4)]
        at += 4 * NG * T * 4
        diag = carve(counts, HG, at, 2 * HG, F32).rearrange("p (h g) -> p h g", h=2)
        dstT = sb("dstT", [P, NG, T])
        srcT = sb("srcT", [P, NG, T], I32)
        keys = sb("keys", [P, NG * T * 4], U8)
        keyT = carve(keys, P, 0, NG * T, I32).rearrange("p (g k) -> p g k", k=T)
        ext = sb("ext", [HG, 2, 4])
        reach = sb("reach", [HG, 3, 2])
        ranges = sb("ranges", [1, 3, NG], I32)
        flag = sb("flag", [1, 1], I32)
        wself = sb("wself", [P, F])
        w1a = sb("w1a", [P, HID])
        w1b = sb("w1b", [P, T, HID])
        w2a = sb("w2a", [P, F])
        w2b = sb("w2b", [HID, F])
        wg = sb("wg", [P, F])
        att_row = sb("att_row", [P, HEADS, 2, HD])
        w3 = sb("w3", [P, 2, F])
        bias = sb("bias", [P, 3, F])
        b0col = sb("b0col", [P, 1])
        x = sb("x", [WIN, NW, F])
        early = sb("early", [P, (NW * F + NPAD) * 4], U8)
        base = carve(early, WIN, 0, NW * F, F32).rearrange("p (w f) -> p w f", w=NW)
        accT = carve(early, P, NW * F * 4, NPAD, F32)
        acc = sb("acc", [WIN, NW, ACCW])
        late = sb("late", [P, NW * 3 * (F + HEADS) * 2], U8)
        parts = {2: carve(late, WIN, 0, NW * 3 * TABW[2], BF16).rearrange("p (w f) -> p w f", w=NW),
                 3: carve(early, WIN, 0, NW * 3 * TABW[3], BF16).rearrange("p (w f) -> p w f", w=NW)}
        small = sb("small", [WIN, 8, CH * HEADS])
        total = sb("total", [P, NI])
        totals = sb("totals", [P, 2])
        idx = sb("idx", [P, SLOTS, T], I32)
        parx = sb("parx", [P, 3, T])
        turns = sb("turns", [P, 18848], U8)
        par = carve(turns, P, 0, NG * 3 * T, F32).rearrange("p (g a k) -> p g a k", a=3, k=T)
        at = NG * 3 * T * 4
        rows = carve(turns, P, at, SLOTS * T * (F + HEADS), F32).rearrange("p (b k f) -> p b k f", b=SLOTS, k=T)
        at += SLOTS * T * (F + HEADS) * 4
        hot = carve(turns, P, at, 2 * T * VW, F32).rearrange("p (a k n) -> p a k n", a=2, k=T)
        at += 2 * T * VW * 4
        parg = carve(turns, P, at, SLOTS * 3 * T, F32).rearrange("p (b a k) -> p b a k", b=SLOTS, a=3)
        cbf = [carve(turns, SB, n * 2 * VW * WIN, VW * WIN, BF16).rearrange("p (h d) -> p h d", h=VW) for n in range(3)]
        cbf_slot = [0, 1, 0, 1, 2]
        keyhot = carve(late, P, 0, 2 * T * (KEYS + 1), BF16).rearrange("p (a k n) -> p a k n", a=2, k=T)
        lohot = carve(late, P, 2 * T * (KEYS + 1) * 2, 2 * T * (SB + 1), BF16).rearrange("p (a k n) -> p a k n", a=2, k=T)
        eas = carve(keys, P, 0, SLOTS * T * R, F32).rearrange("p (b r) -> p b r", b=SLOTS)
        eaT = carve(keys, P, SLOTS * T * R * 4, 2 * P, F32).rearrange("p (a n) -> p a n", a=2)
        f5 = CH * F * 4
        shared = sb("shared", [P, 5 * f5 + CH * (F + HEADS) * 4 + 2 * T * (HID + 1) * 4], U8)
        xn, ta, tb, xT, sT = [carve(shared, q, n * f5, CH * c, F32).rearrange("p (j f) -> p j f", j=CH)
                              for n, (q, c) in enumerate(((WIN, F), (WIN, F), (WIN, F), (P, WIN), (P, WIN)))]
        xs = carve(shared, WIN, 4 * f5, CH * F, F32).rearrange("p (j f) -> p j f", j=CH)
        rest = carve(shared, WIN, f5, CH * (F + HEADS), F32).rearrange("p (j f) -> p j f", j=CH)
        three = carve(shared, WIN, 4 * f5, 3 * (F + HEADS), F32).rearrange("p (a f) -> p a f", a=3)
        tabs = carve(shared, WIN, 5 * f5, CH * (F + HEADS), F32).rearrange("p (j f) -> p j f", j=CH)
        at = 5 * f5 + CH * (F + HEADS) * 4
        hbuf = carve(shared, P, at, 2 * T * (HID + 1), F32).rearrange("p (a k h) -> p a k h", a=2, k=T)
        onehot = carve(shared, P, at, T * WIN, F32).rearrange("p (k n) -> p k n", k=T)

        p0 = ps("p0", [P, 2, 512])
        p1 = ps("p1", [P, 2, 512])
        p2 = ps("p2", [P, 2, 512])
        p3 = ps("p3", [P, 2, 512])
        dense_bank = [p2[0:WIN, j % 2, :] for j in range(CH)]

        tables = [nc.dram_tensor("table_rel", [RELS * N, F], F32),
                  nc.dram_tensor("table_msg", [N, HID], F32),
                  nc.dram_tensor("table_att", [N, F + HEADS], F32),
                  nc.dram_tensor("table_sum", [N, F], F32)]

        def flat(t):
            return t[:, :, :].rearrange("p a n -> p (a n)")

        def win(t, j):
            return t[:, j // 4, P * (j % 4):P * (j % 4) + P]

        s_padded = sem("index_pads_set")
        s_idx_in = sem("indices_in")
        s_w_in = sem("weights_in")
        s_x_in = sem("x_in")
        s_const = sem("constants_made")
        s_set = sem("vector_setup_steps")
        s_cast = sem("indices_cast")
        s_rep = sem("edge_weights_repeated")
        s_reach = sem("reaches_found")
        s_diag = sem("least_destinations_on_a_diagonal")
        s_w1_read = sem("transposed_weights_read")
        s_tr = sem("setup_transposes")
        s_ranges = sem("ranges_ready")
        s_steps = sems("vector_steps", range(5))
        s_xn = sems("x_normalised", range(5))
        s_xtp = sems("x_transposed", range(4))
        s_xts = sems("x_transposed_in_sbuf", range(4))
        s_prod = sems("products", range(4))
        s_tprod = sems("table_products", (0, 1, 3))
        s_prod_read = sems("products_read", range(4))
        s_tab = sems("table_rows_ready", (1, 2, 3))
        s_tabout = sems("table_stored", range(1, 5))
        s_tabfree = sems("table_rows_free", (1, 2, 3))
        s_mprod = sems("sums_transposed_or_multiplied", (1, 2))
        s_mread = sems("sums_made_of_are_read", (1, 2))
        s_nodes = sem("late_node_phases_done")
        s_passed = sem("edge_passes_done")
        s_var = sems("variances", range(1, 5))
        s_root = sems("roots", range(1, 5))
        s_scores = sem("scores_ready")
        s_exp = sem("scores_exped")
        s_even = sem("even_table_windows_copied")
        s_odd = sem("odd_table_windows_copied")
        s_slot = [sem(f"table_slot_stored_{j}") for j in range(CH)]
        s_zeroed = sem("counts_zeroed")
        s_copied = sems("sums_copied", (1, 2))
        s_free = sems("row_slots_free", range(4))
        s_iready = sems("slot_indices", range(4))
        s_rows = [sems(f"rows_in_{l}", range(SLOTS)) for l in range(4)]
        s_hot = sems("onehots", range(4))
        s_visit = sems("visits", range(4))
        s_added = sems("sums_added", range(4))
        s_eas = [sem(f"edge_features_in_{b}") for b in range(SLOTS)]
        s_etp = sem("edge_features_transposed")
        s_ets = sem("edge_features_transposed_in_sbuf")
        s_q = sem("edge_products")
        s_h = sem("messages_steps")
        s_par = sems("slot_keys", (0, 1))
        s_xhot = sems("extra_onehots", (0, 1))
        s_xkeys = sems("extra_keys", (0, 1))
        s_xvisit = sems("extra_visits", (0, 1))
        s_xadded = sems("extra_sums_added", (0, 1))
        s_total = sem("counts_summed")
        s_total_in = sem("totals_by_partition")
        s_total_out = sem("total_of_counts")
        s_flag = sem("flag_ready")
        s_cbf = sems("counts_converted", (2, 3))
        s_pcbf = sems("counts_converted_by_pool", (2, 3))
        s_dense = sems("dense_products", (2, 3))
        s_dread = sems("dense_products_read", (2, 3))
        s_dsum = sems("dense_sums", (2, 3))
        s_pass = {e: sem(f"passed_{e}") for e in ("act", "pool", "dve")}

        def hold(eng, name, s, v):
            eng.wait_ge(s, v)
            eng.sem_inc(s_pass[name])

        def load_range(eng, g):
            return (eng.value_load(ranges[0:1, 0, bass.ds(g, 1)], min_val=0, max_val=NW - 1),
                    eng.value_load(ranges[0:1, 1, bass.ds(g, 1)], min_val=1, max_val=NW))

        def load_packed(eng, g):
            return eng.value_load(ranges[0:1, 2, bass.ds(g, 1)], min_val=PACK, max_val=VISITS * PACK - 1)

        def load_flag(eng):
            return eng.value_load(flag[0:1, 0:1], min_val=0, max_val=1)

        def within(column):
            return nc.s_assert_within(column, 0, N - 1,
                                      skip_runtime_bounds_check_because="a window starts at a node")

        block = ctx.enter_context(nc.Block())

        def edge_loads(sp):
            def load(b, start, parts):
                sp.dma_start(eas[0:parts, b, :],
                             ea[bass.ds(start, parts * T), :].rearrange("(p k) r -> p (k r)", k=T)
                             ).then_inc(s_eas[b], 16)

            with sp.Fori(0, NI - 1) as i:
                for b in range(SLOTS):
                    sp.wait_ge(s_free[1], i * SLOTS + (b + 1))
                    load(b, i * (SLOTS * GE) + b * GE, P)
            for b in range(SLOTS):
                sp.wait_ge(s_free[1], (NI - 1) * SLOTS + b + 1)
                load(b, ((NI - 1) * SLOTS + b) * GE, P if b < SLOTS - 1 else LASTE // T)

        @block.sync
        def _(sp):
            sp.dma_start(x[:, :, :], x_in.rearrange("(w p) f -> p w f", p=WIN)).then_inc(s_x_in, 16)
            sp.wait_ge(s_padded, 1)
            for a, t in enumerate((dst, src, etype)):
                sp.dma_start(stage[:, a, 0, :], t[0:HG * GE].rearrange("(g e) -> g e", e=GE)).then_inc(s_idx_in, 16)
                sp.dma_start(stage[0:HG - 1, a, 1, :],
                             t[HG * GE:(NG - 1) * GE].rearrange("(g e) -> g e", e=GE)).then_inc(s_idx_in, 16)
                sp.dma_start(stage[HG - 1:HG, a, 1, 0:LASTE],
                             t[(NG - 1) * GE:E].rearrange("(a e) -> a e", a=1)).then_inc(s_idx_in, 16)
            sp.dma_start(w0[:, :, :], W0.rearrange("r i o -> i r o")).then_inc(s_w_in, 16)
            sp.dma_start(wself[:, :], Wself).then_inc(s_w_in, 16)
            sp.dma_start(w1raw[:, :], W1).then_inc(s_w_in, 16)
            sp.dma_start(w2raw[:, :], W2).then_inc(s_w_in, 16)
            sp.dma_start(wgraw[:, :], Wg).then_inc(s_w_in, 16)
            sp.dma_start(w3[:, :, :], W3.rearrange("(a i) o -> i a o", a=2)).then_inc(s_w_in, 16)
            sp.dma_start(att_row[:, :, :, :].rearrange("p h a d -> p (h a d)"),
                         att.rearrange("h d -> (h d)").partition_broadcast(P)).then_inc(s_w_in, 16)
            sp.dma_start(b0col[:, :], b0.rearrange("(p a) -> p a", a=1)).then_inc(s_w_in, 16)
            for n, b in enumerate((b2, bg, b3)):
                sp.dma_start(bias[:, n, :], b.partition_broadcast(P)).then_inc(s_w_in, 16)

            for j in range(CH):
                sp.sem_inc(s_slot[j], 16)
            with sp.Fori(0, NC) as c:
                for j in range(CH):
                    if j % 2 == 0:
                        sp.wait_ge(s_even, c * 3 + (j // 2 + 2))
                    else:
                        sp.wait_ge(s_odd, c * 2 + ((j + 1) // 2 + 1))
                    sp.dma_start(tables[0].ap().rearrange("(r n) f -> n r f", r=RELS)
                                 [bass.ds(c * (CH * WIN) + j * WIN, WIN), :, :],
                                 table0[:, j, :].rearrange("p (r f) -> p r f", r=RELS)).then_inc(s_slot[j], 16)

            for n in range(1, 4):
                sp.sem_inc(s_tabfree[n])
                with sp.Fori(0, NC) as c:
                    sp.wait_ge(s_tab[n], c + 1)
                    sp.dma_start(tables[n].ap()[bass.ds(c * (CH * WIN), CH * WIN), :]
                                 .rearrange("(j p) f -> p j f", p=WIN),
                                 tabs[:, :, 0:TABW[n]]).then_inc(s_tabout[n], 16)
                    sp.wait_ge(s_tabout[n], c * 16 + 16)
                    sp.sem_inc(s_tabfree[n])
                if n == 1:
                    edge_loads(sp)
            with sp.Fori(0, NC) as c:
                sp.wait_ge(s_xn[4], c + 1)
                sp.dma_start(out[bass.ds(c * (CH * WIN), CH * WIN), :].rearrange("(j p) f -> p j f", p=WIN),
                             x[:, bass.ds(c * CH, CH), :]).then_inc(s_tabout[4], 16)
            sp.wait_ge(s_tabout[4], 16 * NC)

        @block.gpsimd
        def _(pool):
            pool.memset(ident[:, :], 0.0).then_inc(s_const, 1)
            pool.wait_ge(s_const, 1)
            pool.affine_select(out=ident[:, :], in_=ident[:, :], compare_op=ALU.not_equal, fill=1.0,
                               base=0, pattern=[[-1, P]], channel_multiplier=1).then_inc(s_const, 1)
            pool.iota(iota[:, :], pattern=[[1, WIN]], base=0, channel_multiplier=0,
                      allow_small_or_imprecise_dtypes=True).then_inc(s_const, 1)
            pool.iota(wstart[:, :], pattern=[[WIN, NW]], base=0, channel_multiplier=0,
                      allow_small_or_imprecise_dtypes=True).then_inc(s_const, 1)
            pool.iota(iota16[:, :], pattern=[[1, KEYS + 1]], base=0, channel_multiplier=0,
                      allow_small_or_imprecise_dtypes=True).then_inc(s_const, 1)
            pool.iota(kcode[:, :], pattern=[[-FAR, VISITS]], base=0, channel_multiplier=0,
                      allow_small_or_imprecise_dtypes=True).then_inc(s_const, 1)
            pool.iota(kloc[:, :], pattern=[[-VW, VISITS]], base=0, channel_multiplier=0,
                      allow_small_or_imprecise_dtypes=True).then_inc(s_const, 1)
            pool.memset(ones[:, :], 1.0).then_inc(s_const, 1)
            pool.wait_ge(s_ranges, 1)
            pool.memset(counts[:, LATE:NI * AB].bitcast(I32), 0).then_inc(s_zeroed, 1)

            def gathers(l):
                with pool.Fori(0, NI) as i:
                    for b in range(SLOTS):
                        hold(pool, "pool", s_iready[l], i * SLOTS + (b + 1))
                        for k in range(T):
                            pool.indirect_dma_start(
                                rows[:, b, k, 0:TABW[l]], None, tables[l].ap(),
                                bass.IndirectOffsetOnAxis(ap=idx[:, b, k:k + 1], axis=0),
                            ).then_inc(s_rows[l][b], 16)

            def counts_to_bf16(l):
                if l == 3:
                    pool.wait_ge(s_dense[2], NW + 3)
                with pool.Fori(0, NC) as c:
                    for j in POOLS:
                        hold(pool, "pool", s_dense[l], c * CH + FREED[j])
                        pool.tensor_copy(cbf[cbf_slot[j]], cnt[:, :, bass.ds(c * (CH * WIN) + j * WIN, WIN)]
                                         ).then_inc(s_pcbf[l], 1)

            for j in range(CH):
                pool.wait_ge(s_slot[j], 16 * (NC + 1))
            gathers(0)
            pool.wait_ge(s_copied[1], NC)
            pool.memset(accT[0:HID + 1, :], 0.0).then_inc(s_zeroed, 1)
            pool.wait_ge(s_tabout[1], 16 * NC)
            gathers(1)
            for l in (2, 3):
                pool.wait_ge(s_tabout[l], 16 * NC)
                if l == 2:
                    pool.wait_ge(s_flag, 1)
                pool.wait_ge(s_nodes, l - 1)
                lost = load_flag(pool)
                with pool.If(lost < 1):
                    counts_to_bf16(l)
                with pool.If(lost > 0):
                    gathers(l)

        @block.scalar
        def _(act):
            def to_sbuf(to, frm):
                return act.activation(to, frm, ACT.Copy)

            def transposed_x(n, c):
                act.wait_ge(s_xtp[n], c + 2)
                act.wait_ge(s_prod[n], c + 1)
                to_sbuf(xT[:, :, 0:WIN], flat(p0).rearrange("p (j n) -> p j n", n=P)[:, 0:CH, 0:WIN]
                        ).then_inc(s_xts[n], 1)

            def slot_indices(l, g, b):
                hold(act, "act", s_free[l], g + 1)
                to_sbuf(idx[:, b, :], (keyT if l == 0 else srcT)[:, bass.ds(g, 1), :]
                        .rearrange("p a k -> p (a k)")).then_inc(s_iready[l], 1)

            def edge_pass(l):
                if l == 1:
                    act.wait_ge(s_passed, 1)
                    act.sem_inc(s_total)
                with act.Fori(0, NI) as i:
                    for b in range(SLOTS):
                        g = i * SLOTS + b
                        slot_indices(l, g, b)
                        to_sbuf(parg[:, b, :, :], par[:, bass.ds(g, 1), :, :].rearrange("p a c k -> p (a c) k")
                                ).then_inc(s_par[l], 1)
                        if l == 1:
                            act.wait_ge(s_etp, g + 1)
                            to_sbuf(eaT[:, b % 2, :], p0[:, b % 2, 0:P]).then_inc(s_ets, 1)
                    if l == 1:
                        hold(act, "act", s_total, i + 1)
                        counted = counts[0:SB, bass.ds(i * AB, AB)]
                        act.activation(counted, counted, ACT.Copy,
                                       accum_out=total[0:SB, bass.ds(i, 1)]).then_inc(s_total, 1)

            def slow_pass(l):
                with act.Fori(0, NI) as i:
                    for b in range(SLOTS):
                        slot_indices(l, i * SLOTS + b, b)

            act.sem_inc(s_prod[0])
            act.sem_inc(s_even)
            with act.Fori(0, NC) as c:
                transposed_x(0, c)
                for j in range(0, CH, 2):
                    act.wait_ge(s_tprod[0], c * CH + (j + 1))
                    act.wait_ge(s_slot[j], c * 16 + 16)
                    to_sbuf(table0[:, j, :], flat(p1)[0:WIN, :]).then_inc(s_even, 1)
            edge_pass(0)
            def counts_to_bf16(l, c, j):
                hold(act, "act", s_dense[l], c * CH + FREED[j])
                to_sbuf(cbf[cbf_slot[j]], cnt[:, :, bass.ds(c * (CH * WIN) + j * WIN, WIN)]).then_inc(s_cbf[l], 1)

            def node_chunk(n, c, between=()):
                if n < 3:
                    hold(act, "act", s_mprod[n], c + 1)
                    rws = (P, HID + 1)[n - 1]
                    act.activation(sT[0:rws, :, 0:WIN],
                                   accT[0:rws, bass.ds(c * (CH * WIN), CH * WIN)].rearrange("p (j n) -> p j n", j=CH),
                                   (ACT.Relu, ACT.Copy)[n - 1]).then_inc(s_copied[n], 1)
                for j in between[0:4 if n < 4 else 2]:
                    counts_to_bf16(n - 1, c + 1, j)
                roots = 2 if n == 4 else 1
                if n == 4:
                    act.wait_ge(s_var[n], c * 2 + 1)
                    act.activation(small[:, 5, 0:CH], small[:, 4, 0:CH], ACT.Sqrt).then_inc(s_root[n], 1)
                    for j in between[2:4]:
                        counts_to_bf16(n - 1, c + 1, j)
                act.wait_ge(s_var[n], c * roots + roots)
                act.activation(small[:, 5, 0:CH], small[:, 4, 0:CH], ACT.Sqrt).then_inc(s_root[n], 1)
                if n < 4:
                    transposed_x(n, c)
                if n in (1, 3):
                    act.wait_ge(s_tprod[n], c + 1)
                    act.wait_ge(s_tabfree[n], c + 1)
                    frm = flat(p1)[0:WIN, 0:CH * TABW[n]].rearrange("p (j f) -> p j f", j=CH)
                    to_sbuf(tabs[:, :, 0:TABW[n]], frm).then_inc(s_tab[n], 1)
                if n == 2:
                    act.wait_ge(s_scores, c + 1)
                    act.activation(small[:, 6, :], small[:, 4, :], ACT.Exp).then_inc(s_exp, 1)
                    act.activation(small[:, 7, :], small[:, 5, :], ACT.Exp, scale=-1.0).then_inc(s_exp, 1)

            for n in range(1, 5):
                if n < 4:
                    act.sem_inc(s_prod[n])
                if n < 3:
                    act.wait_ge(s_passed, n)
                    with act.Fori(0, NC) as c:
                        node_chunk(n, c)
                if n == 1:
                    edge_pass(1)
                if n > 2:
                    act.wait_ge(s_nodes, n - 2)
                    lost = load_flag(act)
                    with act.If(lost < 1):
                        for j in ACTS:
                            counts_to_bf16(n - 1, 0, j)
                        with act.Fori(0, NC - 1) as c:
                            node_chunk(n, c, ACTS)
                        node_chunk(n, NC - 1)
                    with act.If(lost > 0):
                        slow_pass(n - 1)
                        with act.Fori(0, NC) as c:
                            node_chunk(n, c)

        @block.tensor
        def _(pe):
            def transpose_x(n, c):
                pe.wait_ge(s_xn[n], c + 1)
                pe.wait_ge(s_xts[n], c + 1)
                for j in range(CH):
                    last = pe.transpose(win(p0, j)[:, 0:WIN], xn[:, j, :], ident[0:WIN, 0:WIN])
                last.then_inc(s_xtp[n], 1)

            def transpose_edges(i, b):
                pe.wait_ge(s_eas[b], i * 16 + 16)
                pe.transpose(p0[:, b % 2, 0:P], eas[:, b, :], ident[:, :]).then_inc(s_etp, 1)
                pe.wait_ge(s_ets, i * SLOTS + (b + 1))
                pe.matmul(p1[:, b % 2, 0:T * HID], eaT[:, b % 2, :],
                          w1b[:, :, :].rearrange("p k h -> p (k h)"), start=True, stop=True).then_inc(s_q, 1)

            def edge_pass(l):
                extra = pe.alloc_register(f"pe_extra_onehots_{l}")
                pe.reg_mov(extra, 0)
                hots, sets = ((HOTS, SETS), (1, 1))[l]

                def count_pairs(par):
                    for k in range(T):
                        pe.matmul(p0[0:SB, par, 0:KEYS - SB], lohot[:, par, k, 0:SB],
                                  keyhot[:, par, k, 0:KEYS - SB], start=(k == 0), stop=(k == T - 1))
                        pe.matmul(p1[0:SB, par, 0:SB], lohot[:, par, k, 0:SB],
                                  keyhot[:, par, k, KEYS - SB:KEYS], start=(k == 0), stop=(k == T - 1))

                def add_rows(b, par):
                    wide = (F, HID + 1)[l]
                    for k in range(T):
                        what = hbuf[:, par, k, :] if l == 1 else rows[:, b, k, 0:F]
                        last = pe.matmul(p2[0:wide, par, 0:VW], what, hot[:, par, k, :],
                                         start=(k == 0), stop=(k == T - 1))
                    return last

                def group(i, b):
                    g, par = i * SLOTS + b, b % 2
                    visits = load_packed(pe, g) // PACK
                    pe.wait_ge(s_hot[l], i * (hots * SLOTS) + hots * (b + 1))
                    pe.wait_ge(s_added[l], i * (sets * SLOTS) + sets * (b + 1))
                    if l == 0:
                        count_pairs(par)
                        pe.wait_ge(s_rows[l][b], i * (16 * T) + 16 * T)
                    else:
                        pe.wait_ge(s_h, i * (2 * SLOTS) + 2 * (b + 1))
                    add_rows(b, par).then_inc(s_visit[l], 1)
                    with pe.If(visits > 1):
                        with pe.Fori(1, visits):
                            pe.reg_add(extra, extra, XHOTS[l])
                            pe.wait_ge(s_xhot[l], pe.snap(extra))
                            if l == 0:
                                count_pairs(par)
                            add_rows(b, par).then_inc(s_xvisit[l], 1)

                if l == 1:
                    transpose_edges(0, 0)
                with pe.Fori(0, NI - 1) as i:
                    for b in range(SLOTS):
                        if l == 1:
                            transpose_edges(*((i, b + 1) if b < SLOTS - 1 else (i + 1, 0)))
                        group(i, b)
                for b in range(SLOTS):
                    if l == 1 and b < SLOTS - 1:
                        transpose_edges(NI - 1, b + 1)
                    group(NI - 1, b)

            def slow_pass(l):
                visits = pe.alloc_register(f"pe_visits_{l}")
                pe.reg_mov(visits, 0)
                wide = SUMW[l]
                with pe.Fori(0, NI) as i:
                    for b in range(SLOTS):
                        pe.wait_ge(s_rows[l][b], i * (16 * T) + 16 * T)
                        lo, hi = load_range(pe, i * SLOTS + b)
                        with pe.Fori(lo, hi):
                            pe.reg_add(visits, visits, 1)
                            v = pe.snap(visits)
                            pe.wait_ge(s_hot[l], v)
                            pe.wait_ge(s_added[l], v)
                            for k in range(T):
                                last = pe.matmul(p2[0:WIN, 0, 0:wide], onehot[:, k, :], rows[:, b, k, 0:wide],
                                                 start=(k == 0), stop=(k == T - 1))
                            last.then_inc(s_visit[l], 1)

            def dense_window(l, c, j):
                wide = 3 * TABW[l]
                if j in POOLS:
                    pe.wait_ge(s_pcbf[l], c * len(POOLS) + (POOLS.index(j) + 1))
                else:
                    pe.wait_ge(s_cbf[l], c * len(ACTS) + (ACTS.index(j) + 1))
                pe.wait_ge(s_dread[l], c * CH + (2, 1, 3, 4, 5)[j])
                for h in range(VW):
                    last = pe.matmul(dense_bank[j][:, 0:wide], cbf[cbf_slot[j]][:, h, :],
                                     parts[l][:, h, 0:wide], start=(h == 0), stop=(h == VW - 1))
                last.then_inc(s_dense[l], 1)

            pe.wait_ge(s_const, 2)
            pe.wait_ge(s_w_in, 16 * 11)
            pe.transpose(win(p3, 0)[:, 0:HID], w1raw[:, 0:F], ident[0:HID, 0:HID])
            pe.transpose(win(p3, 2), w2raw[:, 0:F], ident[:, :])
            pe.transpose(win(p3, 3)[0:HID, :], w2raw[:, F:F + HID], ident[:, :])
            pe.wait_ge(s_rep, 1)
            pe.transpose(win(p3, 1)[:, 0:HID], w1rep[:, :, :].rearrange("h k r -> h (k r)"), ident[0:HID, 0:HID])
            pe.transpose(win(p3, 4), wgraw[:, :], ident[:, :]).then_inc(s_tr, 1)
            pe.wait_ge(s_cast, 3)
            for a in range(3):
                for h in range(2):
                    for k in range(T):
                        last = pe.transpose((p0, p1, p2)[a][:, h, k * HG:(k + 1) * HG],
                                            staged[:, a, h, :].rearrange("g (e k) -> g k e", k=T)[:, k, :],
                                            ident[0:HG, 0:HG])
            pe.wait_ge(s_reach, 1)
            for r in range(3):
                for h in range(2):
                    pe.transpose((p0, p1, p2)[r][0:1, h, T * HG:(T + 1) * HG], reach[:, r, h:h + 1],
                                 ident[0:HG, 0:HG])
            pe.wait_ge(s_diag, 1)
            pe.wait_ge(s_w1_read, 1)
            for h in range(2):
                last = pe.matmul(p3[:, h, 0:HG], ones[0:HG, :], diag[:, h, :], start=True, stop=True)
            last.then_inc(s_tr, 1)
            pe.wait_ge(s_ranges, 1)

            pe.sem_inc(s_xts[0])
            pe.sem_inc(s_xtp[0])
            with pe.Fori(0, NC) as c:
                transpose_x(0, c)
                pe.wait_ge(s_xts[0], c + 2)
                pe.wait_ge(s_prod_read[0], c + 1)
                for j in range(CH):
                    if j % 2 == 0:
                        pe.wait_ge(s_even, c * 3 + (j // 2 + 1))
                    else:
                        pe.wait_ge(s_odd, c * 2 + (j + 1) // 2)
                    for h in range(2):
                        last = pe.matmul((p1, p2)[j % 2][0:WIN, h, :], xT[:, j, 0:WIN],
                                         w0[:, 4 * h:4 * h + 4, :].rearrange("p r f -> p (r f)"),
                                         start=True, stop=True)
                    last.then_inc(s_tprod[0], 1)
                for j in range(CH):
                    last = pe.matmul(win(p3, j)[:, 0:WIN], wself[:, :], xT[:, j, 0:WIN], start=True, stop=True)
                last.then_inc(s_prod[0], 1)
            edge_pass(0)

            def node_chunk(n, c, between=()):
                if n < 3:
                    pe.wait_ge(s_copied[n], c + 1)
                    pe.wait_ge(s_mread[n], c + 1)
                if n == 1:
                    for j in range(CH):
                        last = pe.transpose(win(p2, j)[0:WIN, :], sT[:, j, 0:WIN], ident[:, :])
                    last.then_inc(s_mprod[n], 1)
                if n == 2:
                    for j in range(CH):
                        pe.matmul(win(p2, j)[0:WIN, :], sT[0:HID, j, 0:WIN], w2b[:, :], start=True, stop=True)
                    for j in range(CH):
                        last = pe.matmul(p1[0:WIN, 1, j:j + 1], sT[0:HID + 1, j, 0:WIN],
                                         ident[0:HID + 1, HID:HID + 1], start=True, stop=True)
                    last.then_inc(s_mprod[n], 1)
                for j in between[0:3]:
                    dense_window(n - 1, c + 1, j)
                transpose_x(n, c)
                for j in between[3:4]:
                    dense_window(n - 1, c + 1, j)
                pe.wait_ge(s_xts[n], c + 2)
                pe.wait_ge(s_prod_read[n], c + 1)
                if n in (1, 3):
                    wide, w_tab = TABW[n], (w1a[:, :] if n == 1 else w3[:, 1, :])
                    if n == 1:
                        outs = [p1[0:WIN, 0, j * wide:(j + 1) * wide] for j in range(CH)]
                    else:
                        outs = [win(p1, j)[0:WIN, :] for j in range(CH)]
                    pe.wait_ge(s_tabfree[n], c + 1)
                    for j in range(CH):
                        last = pe.matmul(outs[j], xT[:, j, 0:WIN], w_tab, start=True, stop=True)
                    last.then_inc(s_tprod[n], 1)
                w_own = (None, w2a[:, :], wg[:, :], w3[:, 0, :])[n]
                for j in range(CH):
                    last = pe.matmul(win(p3, j)[0:WIN, :], xT[:, j, 0:WIN], w_own, start=True, stop=True)
                last.then_inc(s_prod[n], 1)
                for j in between[4:5]:
                    dense_window(n - 1, c + 1, j)

            for n in range(1, 5):
                if n < 4:
                    pe.sem_inc(s_xts[n])
                    pe.sem_inc(s_xtp[n])
                if n == 2:
                    pe.wait_ge(s_total_in, 1)
                    pe.matmul(p3[0:1, 0, 0:1], totals[0:SB, 0:1], ones[0:SB, 0:1], start=True, stop=True
                              ).then_inc(s_total_out, 1)
                if n < 3:
                    pe.sem_inc(s_mprod[n])
                    with pe.Fori(0, NC) as c:
                        node_chunk(n, c)
                if n == 1:
                    edge_pass(1)
                if n > 2:
                    pe.wait_ge(s_nodes, n - 2)
                    lost = load_flag(pe)
                    with pe.If(lost < 1):
                        pe.sem_inc(s_dense[n - 1], 3)
                        for j in range(CH):
                            dense_window(n - 1, 0, j)
                        with pe.Fori(0, NC - 1) as c:
                            if n == 3:
                                node_chunk(n, c, range(CH))
                            else:
                                for j in range(CH):
                                    dense_window(n - 1, c + 1, j)
                        if n == 3:
                            node_chunk(n, NC - 1)
                    with pe.If(lost > 0):
                        slow_pass(n - 1)
                        if n == 3:
                            with pe.Fori(0, NC) as c:
                                node_chunk(n, c)

        @block.vector
        def _(dve):
            done = [0]

            def setup(ins):
                done[0] += 1
                ins.then_inc(s_set, 1)
                dve.wait_ge(s_set, done[0])

            setup(dve.memset(stage[:, 0, 1, :], NPAD))
            setup(dve.memset(stage[:, 1:3, 1, :], 0))
            dve.sem_inc(s_padded)
            setup(dve.memset(w1b[:, :, :], 0.0))
            dve.wait_ge(s_w_in, 16 * 11)
            for k in range(T):
                setup(dve.tensor_copy(w1rep[:, k, :], w1raw[:, F:F + R]))
            dve.sem_inc(s_rep)
            dve.wait_ge(s_idx_in, 16 * 9)
            setup(dve.tensor_copy(staged[:, 0:2, :, :], stage[:, 0:2, :, :]))
            setup(dve.scalar_tensor_tensor(staged[:, 2, :, :], stage[:, 2, :, :], float(N), stage[:, 1, :, :],
                                           ALU.mult, ALU.add))
            dve.sem_inc(s_cast, 3)
            dve.wait_ge(s_const, 8)

            def floor_div(to, frm, raw, by):
                setup(dve.tensor_scalar(raw, frm, -(by - 1) / 2, 1.0 / by, ALU.add, ALU.mult))
                setup(dve.tensor_scalar(raw, raw, 12582912.0, None, ALU.add))
                setup(dve.tensor_scalar(to, raw, -12582912.0, None, ALU.add))

            setup(dve.tensor_reduce(ext[:, :, 0], staged[:, 0, :, :], X, ALU.min))
            setup(dve.tensor_reduce(ext[:, :, 1], staged[:, 0, :, :], X, ALU.max))
            setup(dve.tensor_scalar(ext[:, :, 1], ext[:, :, 1], N - 1.0, None, ALU.min))
            for h in range(2):
                setup(dve.tensor_scalar(diag[:, h, :], ident[0:HG, 0:HG], ext[:, h, 0:1], None, ALU.mult))
            dve.sem_inc(s_diag)
            floor_div(reach[:, 0, :], ext[:, :, 0], ext[:, :, 2], WIN)
            floor_div(reach[:, 1, :], ext[:, :, 1], ext[:, :, 2], WIN)
            setup(dve.tensor_scalar(reach[:, 1, :], reach[:, 1, :], 1.0, None, ALU.add))
            setup(dve.tensor_tensor(ext[:, :, 3], ext[:, :, 1], ext[:, :, 0], ALU.subtract))
            floor_div(ext[:, :, 3], ext[:, :, 3], ext[:, :, 2], VW)
            setup(dve.tensor_scalar(ext[:, :, 3], ext[:, :, 3], 1.0, float(PACK), ALU.add, ALU.mult))
            setup(dve.tensor_tensor(reach[:, 2, :], ext[:, :, 3], ext[:, :, 0], ALU.add))
            dve.sem_inc(s_reach)
            dve.wait_ge(s_tr, 1)
            setup(dve.tensor_copy(w1a[:, :], win(p3, 0)[:, 0:HID]))
            for k in range(T):
                setup(dve.tensor_copy(w1b[R * k:R * k + R, k, :], win(p3, 1)[R * k:R * k + R, 0:HID]))
            setup(dve.tensor_copy(w2a[:, :], win(p3, 2)))
            setup(dve.tensor_copy(w2b[:, :], win(p3, 3)[0:HID, :]))
            setup(dve.tensor_copy(wg[:, :], win(p3, 4)))
            dve.sem_inc(s_w1_read)
            dve.wait_ge(s_tr, 2)
            for a, to in enumerate((dstT, srcT, keyT)):
                for h in range(2):
                    setup(dve.tensor_copy(to[:, h * HG:(h + 1) * HG, :].rearrange("p g k -> p k g"),
                                          (p0, p1, p2)[a][:, h, 0:T * HG].rearrange("p (k g) -> p k g", k=T)))
            for r in range(3):
                for h in range(2):
                    setup(dve.tensor_copy(ranges[0:1, r, h * HG:(h + 1) * HG],
                                          (p0, p1, p2)[r][0:1, h, T * HG:(T + 1) * HG]))
            for h in range(2):
                gs = slice(h * HG, (h + 1) * HG)
                setup(dve.tensor_tensor(setf[0][:, gs, :], dstT[:, gs, :],
                                        p3[:, h, 0:HG].unsqueeze(2).to_broadcast([P, HG, T]), ALU.subtract))
            setup(dve.tensor_copy(par[:, :, 2, :], setf[0]))
            setup(dve.tensor_copy(setf[1], srcT[:, :, :]))
            floor_div(setf[2], setf[1], setf[3], SB)
            setup(dve.scalar_tensor_tensor(par[:, :, 1, :], setf[2], -float(SB), setf[1], ALU.mult, ALU.add))
            setup(dve.scalar_tensor_tensor(setf[1], setf[2], float(VW), setf[0], ALU.mult, ALU.add))
            floor_div(setf[2], setf[0], setf[3], VW)
            setup(dve.scalar_tensor_tensor(par[:, :, 0, :], setf[2], float(FAR - VW), setf[1], ALU.mult, ALU.add))
            setup(dve.memset(accT[:, N:NPAD], 0.0))
            dve.wait_ge(s_x_in, 16)
            dve.sem_inc(s_ranges)

            def wide(t):
                return flat(t)[0:WIN, 0:CH * F].rearrange("p (j f) -> p j f", j=CH)

            def over(t, shape):
                return t.to_broadcast(shape)

            def biased(n):
                return bias[0:WIN, n:n + 1, :].to_broadcast([WIN, CH, F])

            def col(n):
                return small[:, n, 0:CH]

            def each(n):
                return col(n).unsqueeze(2).to_broadcast([WIN, CH, F])

            def start_nodes(n):
                if n < 4:
                    dve.sem_inc(s_prod_read[n])
                if n == 0:
                    dve.sem_inc(s_odd)
                if n in (1, 2):
                    dve.sem_inc(s_mread[n])

            def node_chunk(n, c, between=None):
                steps = [0]
                roots = 2 if n == 4 else 1

                def step(ins):
                    steps[0] += 1
                    ins.then_inc(s_steps[n], 1)
                    dve.wait_ge(s_steps[n], c * STEPS[n] + steps[0])
                    if between and steps[0] in ADDS_AFTER[n]:
                        between(ADDS_AFTER[n].index(steps[0]))

                xc = x[:, bass.ds(c * CH, CH), :]
                ac = acc[:, bass.ds(c * CH, CH), :]
                bc = base[:, bass.ds(c * CH, CH), :]
                if n == 1:
                    dve.wait_ge(s_mprod[n], c + 2)
                    step(dve.tensor_tensor(ta[:, :, :], wide(p2), xc, ALU.add))
                    dve.sem_inc(s_mread[n])
                if n == 2:
                    dve.wait_ge(s_mprod[n], c + 2)
                    step(dve.tensor_scalar(col(0), p1[0:WIN, 1, 0:CH], 1.0, None, ALU.max))
                    step(dve.reciprocal(col(1), col(0)))
                    step(dve.tensor_tensor(tb[:, :, :], wide(p2), each(1), ALU.mult))
                    dve.sem_inc(s_mread[n])
                    step(dve.tensor_tensor(tb[:, :, :], tb[:, :, :], bc, ALU.add))
                    step(dve.scalar_tensor_tensor(ta[:, :, :], tb[:, :, :], 0.01, tb[:, :, :], ALU.mult, ALU.max))
                    step(dve.tensor_tensor(ta[:, :, :], ta[:, :, :], xc, ALU.add))
                if n == 3:
                    s5 = small[:, 0, :].rearrange("p (j h) -> p j h", j=CH)
                    s6 = small[:, 1, :].rearrange("p (j h) -> p j h", j=CH)
                    step(dve.tensor_tensor(s5, ac[:, :, F:F + HEADS], ac[:, :, F + HEADS:F + 2 * HEADS], ALU.add))
                    step(dve.reciprocal(s6, s5))
                    for h in range(HEADS):
                        cols = slice(h * HD, (h + 1) * HD)
                        step(dve.tensor_tensor(ta[:, :, cols], ac[:, :, cols],
                                               s6[:, :, h:h + 1].to_broadcast([WIN, CH, HD]), ALU.mult))
                    step(dve.tensor_tensor(ta[:, :, :], ta[:, :, :], biased(1), ALU.add))
                    step(dve.tensor_tensor(ta[:, :, :], ta[:, :, :], xc, ALU.add))
                if n == 4:
                    step(dve.tensor_scalar(ta[:, :, :], ac[:, :, 0:F], 0.0, None, ALU.max))
                    step(dve.tensor_tensor(tb[:, :, :], ta[:, :, :], ta[:, :, :], ALU.mult))
                    step(dve.tensor_reduce(col(0), tb[:, :, :], X, ALU.add))
                    step(dve.tensor_scalar(col(4), col(0), 1e-24, None, ALU.max))
                    dve.sem_inc(s_var[n])
                    dve.wait_ge(s_root[n], c * 2 + 1)
                    step(dve.reciprocal(col(1), col(5)))
                    step(dve.tensor_tensor(ta[:, :, :], ta[:, :, :], each(1), ALU.mult))
                    step(dve.tensor_tensor(ta[:, :, :], ta[:, :, :], xc, ALU.add))
                if n > 0:
                    step(dve.tensor_reduce(col(2), ta[:, :, :], X, ALU.add))
                    step(dve.tensor_scalar(col(3), col(2), 1.0 / F, None, ALU.mult))
                    step(dve.tensor_tensor(ta[:, :, :], ta[:, :, :], each(3), ALU.subtract))
                    step(dve.tensor_tensor(tb[:, :, :], ta[:, :, :], ta[:, :, :], ALU.mult))
                    step(dve.tensor_reduce(col(0), tb[:, :, :], X, ALU.add))
                    step(dve.tensor_scalar(col(4), col(0), 1.0 / F, EPS, ALU.mult, ALU.add))
                    dve.sem_inc(s_var[n])
                    dve.wait_ge(s_root[n], c * roots + roots)
                    step(dve.reciprocal(col(2), col(5)))
                if n == 4:
                    dve.tensor_tensor(xc, ta[:, :, :], each(2), ALU.mult).then_inc(s_xn[4], 1)
                    step(dve.tensor_copy(col(6), col(2)))
                elif n > 0:
                    dve.wait_ge(s_xtp[n], c + 1)
                    step(dve.tensor_tensor(xn[:, :, :], ta[:, :, :], each(2), ALU.mult))
                    dve.sem_inc(s_xn[n])
                    step(dve.tensor_copy(xc, xn[:, :, :]))
                else:
                    dve.wait_ge(s_xtp[n], c + 1)
                    step(dve.tensor_copy(xn[:, :, :], xc))
                    dve.sem_inc(s_xn[n])
                if n == 0:
                    for j in range(1, CH, 2):
                        dve.wait_ge(s_tprod[0], c * CH + (j + 1))
                        dve.wait_ge(s_slot[j], c * 16 + 16)
                        dve.tensor_copy(table0[:, j, :], flat(p2)[0:WIN, :]).then_inc(s_odd, 1)
                if n < 4:
                    dve.wait_ge(s_prod[n], c + 2)
                if n == 0:
                    step(dve.tensor_scalar(
                        accT[:, bass.ds(c * (CH * WIN), CH * WIN)].rearrange("p (j n) -> p j n", j=CH),
                        flat(p3).rearrange("p (j n) -> p j n", n=P)[:, 0:CH, 0:WIN], b0col[:, 0:1], None, ALU.add))
                    dve.sem_inc(s_prod_read[n])
                if n == 1:
                    step(dve.tensor_tensor(bc, wide(p3), biased(0), ALU.add))
                    dve.sem_inc(s_prod_read[n])
                if n == 2:
                    step(dve.tensor_copy(ta[:, :, :], wide(p3)))
                    dve.sem_inc(s_prod_read[n])
                    step(dve.scalar_tensor_tensor(tb[:, :, :], ta[:, :, :], 0.2, ta[:, :, :], ALU.mult, ALU.max))
                    for a in range(2):
                        for h in range(HEADS):
                            step(dve.tensor_tensor(
                                xs[:, :, h * HD:(h + 1) * HD], tb[:, :, h * HD:(h + 1) * HD],
                                att_row[0:WIN, h, a:a + 1, :].to_broadcast([WIN, CH, HD]), ALU.mult))
                        step(dve.tensor_reduce(small[:, 4 + a, :],
                                               xs[:, :, :].rearrange("p j (h d) -> p (j h) d", h=HEADS),
                                               X, ALU.add))
                    dve.sem_inc(s_scores)
                    dve.wait_ge(s_exp, c * 2 + 2)
                    dve.wait_ge(s_tabfree[n], c + 1)
                    e = small[:, 6, :].rearrange("p (j h) -> p j h", j=CH)
                    step(dve.tensor_copy(tabs[:, :, F:F + HEADS], e))
                    for h in range(HEADS):
                        cols = slice(h * HD, (h + 1) * HD)
                        step(dve.tensor_tensor(tabs[:, :, cols], ta[:, :, cols],
                                               e[:, :, h:h + 1].to_broadcast([WIN, CH, HD]), ALU.mult))
                    dve.sem_inc(s_tab[n])
                    step(dve.tensor_copy(ac[:, :, 0:F + HEADS], tabs[:, :, :]))
                    step(dve.tensor_scalar(ac[:, :, F + HEADS:F + 2 * HEADS],
                                           small[:, 7, :].rearrange("p (j h) -> p j h", j=CH),
                                           1e-9, None, ALU.mult))
                if n == 3:
                    step(dve.tensor_tensor(ac[:, :, 0:F], wide(p3), biased(2), ALU.add))
                    dve.sem_inc(s_prod_read[n])
                    dve.wait_ge(s_tab[n], c + 1)
                if n in (2, 3):
                    wd = TABW[n]
                    part = [parts[n][:, bass.ds(c * CH, CH), m * wd:(m + 1) * wd] for m in range(3)]
                    step(dve.tensor_copy(part[0], tabs[:, :, 0:wd]))
                    step(dve.tensor_tensor(rest[:, :, 0:wd], tabs[:, :, 0:wd], part[0], ALU.subtract))
                    step(dve.tensor_copy(part[1], rest[:, :, 0:wd]))
                    step(dve.tensor_tensor(rest[:, :, 0:wd], rest[:, :, 0:wd], part[1], ALU.subtract))
                    step(dve.tensor_copy(part[2], rest[:, :, 0:wd]))
                assert steps[0] == STEPS[n], (n, steps[0])

            def edge_pass(l):
                counted = {e: dve.alloc_register(f"dve_extra_{e}_{l}") for e in ("keys", "visits", "sums")}
                sets = (SETS, 1)[l]
                feats = (F, HID + 1)[l]

                def count(what, by):
                    dve.reg_add(counted[what], counted[what], by)
                    return dve.snap(counted[what])

                def onehots(par, keys, sources, places, s_built):
                    if l == 0:
                        for k in range(T):
                            dve.tensor_scalar(keyhot[:, par, k, :], iota16[:, :], keys[:, k:k + 1], None,
                                              ALU.is_equal).then_inc(s_built, 1)
                        if sources is not None:
                            for k in range(T):
                                dve.tensor_scalar(lohot[:, par, k, :], iota16[:, 0:SB + 1], sources[:, k:k + 1], None,
                                                  ALU.is_equal).then_inc(s_built, 1)
                    dve.tensor_tensor(hot[:, par, :, :], iota[:, 0:VW].unsqueeze(1).to_broadcast([P, T, VW]),
                                      places.unsqueeze(2).to_broadcast([P, T, VW]), ALU.is_equal).then_inc(s_built, 1)

                def build(i, b):
                    par = b % 2
                    dve.wait_ge(s_par[l], i * SLOTS + (b + 1))
                    onehots(par, parg[:, b, 0, :], parg[:, b, 1, :], parg[:, b, 2, :], s_hot[l])
                    if l == 1:
                        dve.wait_ge(s_rows[l][b], i * (16 * T) + 16 * T)
                        dve.wait_ge(s_q, i * SLOTS + (b + 1))
                        dve.tensor_tensor(hbuf[:, par, :, 0:HID],
                                          p1[:, par, 0:T * HID].rearrange("p (k h) -> p k h", k=T),
                                          rows[:, b, :, 0:HID], ALU.add).then_inc(s_h, 1)
                        dve.wait_ge(s_h, i * (2 * SLOTS) + (2 * b + 1))
                        dve.scalar_tensor_tensor(hbuf[:, par, :, 0:HID], hbuf[:, par, :, 0:HID], 0.01,
                                                 hbuf[:, par, :, 0:HID], ALU.mult, ALU.max).then_inc(s_h, 1)

                def add(par, first, s_done):
                    cols = accT[0:feats, bass.ds(first, VW)]
                    dve.tensor_tensor(cols, cols, p2[0:feats, par, 0:VW], ALU.add).then_inc(s_done, 1)
                    if l == 0:
                        for blocks, bank in ((slice(0, VW - CH), p0[0:SB, par, 0:KEYS - SB]),
                                             (slice(VW - CH, VW), p1[0:SB, par, 0:SB])):
                            pairs = cnt[:, blocks, bass.ds(first, VW)]
                            dve.tensor_tensor(pairs, pairs, bank.rearrange("p (h d) -> p h d", d=VW), ALU.add
                                              ).then_inc(s_done, 1)

                def group(i, b, after):
                    g, par = i * SLOTS + b, b % 2
                    packed = load_packed(dve, g)
                    first, visits = packed % PACK, packed // PACK
                    if after is not None:
                        build(*after)
                    dve.wait_ge(s_visit[l], g + 1)
                    dve.wait_ge(s_added[l], i * (sets * SLOTS) + sets * (b + 2))
                    add(par, within(first), s_added[l])
                    with dve.If(visits > 1):
                        hold(dve, "dve", s_added[l], i * (sets * SLOTS) + sets * (b + 3))
                        with dve.Fori(1, visits) as k:
                            for a, by in ((0, kcode), (2, kloc)):
                                dve.tensor_scalar(parx[:, a, :], parg[:, b, a, :], by[:, bass.ds(k, 1)], None, ALU.add
                                                  ).then_inc(s_xkeys[l], 1)
                            hold(dve, "dve", s_xkeys[l], count("keys", 2))
                            onehots(par, parx[:, 0, :], None, parx[:, 2, :], s_xhot[l])
                            hold(dve, "dve", s_xvisit[l], count("visits", 1))
                            add(par, within(first + k * VW), s_xadded[l])
                            hold(dve, "dve", s_xadded[l], count("sums", sets))
                    dve.sem_inc(s_free[l])

                for r in counted.values():
                    dve.reg_mov(r, 0)
                dve.sem_inc(s_added[l], 2 * sets)
                if l == 0:
                    for j in range(CH):
                        dve.wait_ge(s_slot[j], 16 * (NC + 1))
                    setup(dve.memset(counts[:, 0:LATE].bitcast(I32), 0))
                    dve.wait_ge(s_zeroed, 1)
                else:
                    dve.wait_ge(s_tabout[1], 16 * NC)
                    setup(dve.memset(hbuf[:, :, :, HID], 1.0))
                    dve.wait_ge(s_zeroed, 2)
                dve.sem_inc(s_free[l], SLOTS)
                build(0, 0)
                with dve.Fori(0, NI - 1) as i:
                    for b in range(SLOTS):
                        group(i, b, (i, b + 1) if b < SLOTS - 1 else (i + 1, 0))
                for b in range(SLOTS):
                    group(NI - 1, b, (NI - 1, b + 1) if b < SLOTS - 1 else None)
                dve.wait_ge(s_added[l], sets * (NG + 2))
                dve.sem_inc(s_passed)

            def find_flag():
                dve.wait_ge(s_total, NI + 1)
                setup(dve.tensor_reduce(totals[0:SB, 0:1], total[0:SB, :], X, ALU.add))
                dve.sem_inc(s_total_in)
                dve.wait_ge(s_total_out, 1)
                setup(dve.tensor_scalar(flag[0:1, 0:1], p3[0:1, 0, 0:1], E - 0.5, None, ALU.is_lt))
                dve.sem_inc(s_flag)

            def slow_pass(l):
                visits = dve.alloc_register(f"dve_visits_{l}")
                wd = SUMW[l]
                dve.sem_inc(s_free[l], SLOTS)
                dve.sem_inc(s_added[l])
                dve.reg_mov(visits, 0)
                with dve.Fori(0, NI) as i:
                    for b in range(SLOTS):
                        g = i * SLOTS + b
                        lo, hi = load_range(dve, g)
                        with dve.Fori(lo, hi) as w:
                            dve.reg_add(visits, visits, 1)
                            v = dve.snap(visits)
                            dve.scalar_tensor_tensor(
                                onehot[:, :, :], iota[:, :].unsqueeze(1).to_broadcast([P, T, WIN]),
                                wstart[:, bass.ds(w, 1)],
                                dstT[:, bass.ds(g, 1), :].rearrange("p a k -> p (a k)").unsqueeze(2)
                                .to_broadcast([P, T, WIN]), ALU.add, ALU.is_equal).then_inc(s_hot[l], 1)
                            dve.wait_ge(s_visit[l], v)
                            dve.wait_ge(s_added[l], v)
                            aw = acc[:, bass.ds(w, 1), 0:wd].rearrange("p a f -> p (a f)")
                            dve.tensor_tensor(aw, aw, p2[0:WIN, 0, 0:wd], ALU.add).then_inc(s_added[l], 1)
                        dve.sem_inc(s_free[l])
                hold(dve, "dve", s_added[l], dve.snap(visits) + 1)

            def dense_add(l, c, j):
                wd = TABW[l]
                dve.wait_ge(s_dense[l], c * CH + (j + 4))
                dve.wait_ge(s_dsum[l], c * CH + (j + 1))
                dve.tensor_reduce(three[:, j % 3, 0:wd], dense_bank[j][:, 0:3 * wd].rearrange("p (m f) -> p f m", m=3),
                                  X, ALU.add).then_inc(s_dread[l], 1)
                dve.wait_ge(s_dread[l], c * CH + (j + 3))
                aw = acc[:, bass.ds(c * CH + j, 1), 0:wd].rearrange("p a f -> p (a f)")
                dve.tensor_tensor(aw, aw, three[:, j % 3, 0:wd], ALU.add).then_inc(s_dsum[l], 1)

            def dense_chunk(l, c):
                for j in range(CH):
                    dense_add(l, c, j)

            for n in range(5):
                start_nodes(n)
                if n < 3:
                    with dve.Fori(0, NC) as c:
                        node_chunk(n, c)
                if n in (0, 1):
                    edge_pass(n)
                if n == 1:
                    find_flag()
                if n > 2:
                    l = n - 1
                    lost = load_flag(dve)
                    with dve.If(lost < 1):
                        dve.sem_inc(s_dread[l], 2)
                        dve.sem_inc(s_dsum[l], 2)
                        dense_chunk(l, 0)
                        with dve.Fori(0, NC - 1) as c:
                            hold(dve, "dve", s_dsum[l], c * CH + (CH + 2))
                            node_chunk(n, c, lambda j: dense_add(l, c + 1, j))
                        dve.wait_ge(s_dsum[l], NW + 2)
                        node_chunk(n, NC - 1)
                    with dve.If(lost > 0):
                        slow_pass(l)
                        with dve.Fori(0, NC) as c:
                            node_chunk(n, c)
                if n in (2, 3):
                    dve.sem_inc(s_nodes)


_INS = ["x", "src", "dst", "edge_attr_32", "edge_type_8", "L0_gnn_weight", "L0_gnn_self_loop_weight",
        "L0_gnn_bias", "L1_gnn_W1", "L1_gnn_W2", "L1_gnn_b2", "L2_gnn_W", "L2_gnn_att", "L2_gnn_bias",
        "L3_gnn_W", "L3_gnn_b"]


def kernel(**inputs):
    import numpy as _np
    import concourse.bacc as _bacc
    from concourse import mybir as _mybir
    from concourse.bass_utils import run_bass_kernel_spmd as _run

    nc = _bacc.Bacc("TRN2", target_bir_lowering=False, num_devices=1)
    arrays, args = {}, []
    for name in _INS:
        a = _np.ascontiguousarray(inputs[name])
        arrays[f"in_{name}"] = a
        args.append(nc.dram_tensor(f"in_{name}", a.shape, _mybir.dt.from_np(a.dtype), kind="ExternalInput").ap())
    args.append(nc.dram_tensor("out_0", (3125, 128), _mybir.dt.float32, kind="ExternalOutput").ap())
    resgnn(nc, *args)
    r = _run(nc, [arrays], core_ids=[0])
    return r.results[0]["out_0"]
```

```python
import concourse.bass as bass
from concourse import mybir
from contextlib import ExitStack

F32 = mybir.dt.float32
I32 = mybir.dt.int32
BF16 = mybir.dt.bfloat16
F16 = mybir.dt.float16
U8 = mybir.dt.uint8
ALU = mybir.AluOpType
ACT = mybir.ActivationFunctionType
X = mybir.AxisListType.X

P = 128
N = 3125
F = 128
E = 100000
RELS = 8
R = 32
HID = 80
HEADS, HD = 4, 32
WIN = 125
NW = N // WIN
CH = 5
NC = NW // CH
T = 4
GE = P * T
NG = -(-E // GE)
SLOTS = 4
NI = NG // SLOTS
VW = 25
SB = N // VW
NPAD = N + VW
VISITS = N // VW + 1
KEYS = VW * VW
FAR = 1024
PACK = 4096
AB = 1608
HOTS = 2 * T + 1
SETS = 3
XHOTS = [T + 1, 1]
HG = NG // 2
LASTE = E - (NG - 1) * GE
ACCW = 136
TABW = [F, HID, F + HEADS, F]
SUMW = [F, HID + 1, F + HEADS, F]
EPS = 1e-5
READ = (2, 1, 3, 4, 5)
FREED = (1, 2, 4, 5, 3)
POOLS = (4,)
ACTS = (0, 1, 2, 3)
STEPS = {1: (8, 1), 2: (13, 8), 3: (12, 6), 4: (13, 0)}
ADDS_AFTER = {3: ((3, 6, 12), (2, 5)), 4: ((2, 6, 9, 12, 13), ())}


def resgnn(nc, x_in, src, dst, ea, etype, W0, Wself, b0, W1, W2, b2, Wg, att, bg, W3, b3, out):
    ctx = ExitStack()
    with ctx:
        def sb(name, shape, dt=F32):
            return ctx.enter_context(nc.sbuf_tensor(name, shape, dt))

        def ps(name, shape):
            return ctx.enter_context(nc.psum_tensor(name, shape, F32))

        def sem(name):
            return ctx.enter_context(nc.semaphore(name))

        def sems(name, which):
            return {n: sem(f"{name}_{n}") for n in which}

        def carve(buf, parts, at, cols, dt):
            size = cols * (4 if dt in (F32, I32) else 2)
            return buf[0:parts, at:at + size].bitcast(dt)

        ident = sb("ident", [P, P])
        iota = sb("iota", [P, WIN])
        iota16 = sb("iota16", [P, KEYS + 1], F16)
        kcode = sb("kcode", [P, VISITS])
        kloc = sb("kloc", [P, VISITS])
        ones = sb("ones", [P, P])
        wstart = sb("wstart", [P, NW])
        counts = sb("counts", [P, NI * AB], U8)
        cnt = counts[0:SB, 0:VW * NPAD].rearrange("p (h d) -> p h d", h=VW)
        table0 = carve(counts, WIN, 0, CH * RELS * F, F32).rearrange("p (s n) -> p s n", s=CH)
        at = CH * RELS * F * 4
        w0 = carve(counts, P, at, RELS * F, F32).rearrange("p (r f) -> p r f", r=RELS)
        at += RELS * F * 4
        LATE = at
        stage = carve(counts, HG, at, 6 * GE, I32).rearrange("p (a h e) -> p a h e", a=3, h=2)
        at += 6 * GE * 4
        staged = carve(counts, HG, at, 6 * GE, F32).rearrange("p (a h e) -> p a h e", a=3, h=2)
        at += 6 * GE * 4
        w1raw = carve(counts, HID, at, F + R, F32)
        w1rep = carve(counts, HID, at + 1024, T * R, F32).rearrange("p (k r) -> p k r", k=T)
        w2raw = carve(counts, P, at + 2048, F + HID, F32)
        wgraw = carve(counts, P, at + 3072, F, F32)
        at += 4096
        setf = [carve(counts, P, at + n * NG * T * 4, NG * T, F32).rearrange("p (g k) -> p g k", k=T)
                for n in range(4)]
        at += 4 * NG * T * 4
        diag = carve(counts, HG, at, 2 * HG, F32).rearrange("p (h g) -> p h g", h=2)
        dstT = sb("dstT", [P, NG, T])
        srcT = sb("srcT", [P, NG, T], I32)
        keys = sb("keys", [P, NG * T * 4], U8)
        keyT = carve(keys, P, 0, NG * T, I32).rearrange("p (g k) -> p g k", k=T)
        ext = sb("ext", [HG, 2, 4])
        reach = sb("reach", [HG, 3, 2])
        ranges = sb("ranges", [1, 3, NG], I32)
        flag = sb("flag", [1, 1], I32)
        wself = sb("wself", [P, F])
        w1a = sb("w1a", [P, HID])
        w1b = sb("w1b", [P, T, HID])
        w2a = sb("w2a", [P, F])
        w2b = sb("w2b", [HID, F])
        wg = sb("wg", [P, F])
        att_row = sb("att_row", [P, HEADS, 2, HD])
        w3 = sb("w3", [P, 2, F])
        bias = sb("bias", [P, 3, F])
        b0col = sb("b0col", [P, 1])
        x = sb("x", [WIN, NW, F])
        early = sb("early", [P, (NW * F + NPAD) * 4], U8)
        base = carve(early, WIN, 0, NW * F, F32).rearrange("p (w f) -> p w f", w=NW)
        accT = carve(early, P, NW * F * 4, NPAD, F32)
        acc = sb("acc", [WIN, NW, ACCW])
        late = sb("late", [P, NW * 3 * (F + HEADS) * 2], U8)
        parts = {2: carve(late, WIN, 0, NW * 3 * TABW[2], BF16).rearrange("p (w f) -> p w f", w=NW),
                 3: carve(early, WIN, 0, NW * 3 * TABW[3], BF16).rearrange("p (w f) -> p w f", w=NW)}
        small = sb("small", [WIN, 8, CH * HEADS])
        total = sb("total", [P, NI])
        warmed = sb("warmed", [1, 1])
        eps = sb("eps", [WIN, 1])
        totals = sb("totals", [P, 2])
        idx = sb("idx", [P, SLOTS, T], I32)
        parx = sb("parx", [P, 3, T])
        turns = sb("turns", [P, 18848], U8)
        par = carve(turns, P, 0, NG * 3 * T, F32).rearrange("p (g a k) -> p g a k", a=3, k=T)
        at = NG * 3 * T * 4
        rows = carve(turns, P, at, SLOTS * T * (F + HEADS), F32).rearrange("p (b k f) -> p b k f", b=SLOTS, k=T)
        at += SLOTS * T * (F + HEADS) * 4
        hot = carve(turns, P, at, 2 * T * VW, F32).rearrange("p (a k n) -> p a k n", a=2, k=T)
        at += 2 * T * VW * 4
        parg = carve(turns, P, at, SLOTS * 3 * T, F32).rearrange("p (b a k) -> p b a k", b=SLOTS, a=3)
        cbf = [carve(turns, SB, n * 2 * VW * WIN, VW * WIN, BF16).rearrange("p (h d) -> p h d", h=VW) for n in range(3)]
        cbf_slot = [0, 1, 0, 1, 2]
        keyhot = carve(late, P, 0, 2 * T * (KEYS + 1), BF16).rearrange("p (a k n) -> p a k n", a=2, k=T)
        lohot = carve(late, P, 2 * T * (KEYS + 1) * 2, 2 * T * (SB + 1), BF16).rearrange("p (a k n) -> p a k n", a=2, k=T)
        eas = carve(keys, P, 0, SLOTS * T * R, F32).rearrange("p (b r) -> p b r", b=SLOTS)
        eaT = carve(keys, P, SLOTS * T * R * 4, 2 * P, F32).rearrange("p (a n) -> p a n", a=2)
        left = carve(keys, WIN, 0, CH * (F + HEADS), F32).rearrange("p (j f) -> p j f", j=CH)
        own = carve(turns, WIN, 2 * 2 * VW * WIN, CH * F, F32).rearrange("p (j f) -> p j f", j=CH)
        f5 = CH * F * 4
        shared = sb("shared", [P, 5 * f5 + CH * (F + HEADS) * 4 + 2 * T * (HID + 1) * 4], U8)
        xn, ta, tb, xT, sT = [carve(shared, q, n * f5, CH * c, F32).rearrange("p (j f) -> p j f", j=CH)
                              for n, (q, c) in enumerate(((WIN, F), (WIN, F), (WIN, F), (P, WIN), (P, WIN)))]
        rest = carve(shared, WIN, f5, CH * (F + HEADS), F32).rearrange("p (j f) -> p j f", j=CH)
        three = carve(shared, WIN, 4 * f5, 3 * (F + HEADS), F32).rearrange("p (a f) -> p a f", a=3)
        tabs = carve(shared, WIN, 5 * f5, CH * (F + HEADS), F32).rearrange("p (j f) -> p j f", j=CH)
        at = 5 * f5 + CH * (F + HEADS) * 4
        xs = carve(shared, WIN, at, CH * F, F32).rearrange("p (j f) -> p j f", j=CH)
        hbuf = carve(shared, P, at, 2 * T * (HID + 1), F32).rearrange("p (a k h) -> p a k h", a=2, k=T)
        onehot = carve(shared, P, at, T * WIN, F32).rearrange("p (k n) -> p k n", k=T)

        p0 = ps("p0", [P, 2, 512])
        p1 = ps("p1", [P, 2, 512])
        p2 = ps("p2", [P, 2, 512])
        p3 = ps("p3", [P, 2, 512])
        dense_bank = [p2[0:WIN, j % 2, :] for j in range(CH)]

        tables = [nc.dram_tensor("table_rel", [RELS * N, F], F32),
                  nc.dram_tensor("table_msg", [N, HID], F32),
                  nc.dram_tensor("table_att", [N, F + HEADS], F32),
                  nc.dram_tensor("table_sum", [N, F], F32)]

        def flat(t):
            return t[:, :, :].rearrange("p a n -> p (a n)")

        def win(t, j):
            return t[:, j // 4, P * (j % 4):P * (j % 4) + P]

        s_padded = sem("index_pads_set")
        s_idx_in = sem("indices_in")
        s_w_in = sem("weights_in")
        s_x_in = sem("x_in")
        s_const = sem("constants_made")
        s_set = sem("vector_setup_steps")
        s_warm = sem("function_tables_loaded")
        s_cast = sem("indices_cast")
        s_rep = sem("edge_weights_repeated")
        s_reach = sem("reaches_found")
        s_diag = sem("least_destinations_on_a_diagonal")
        s_w1_read = sem("transposed_weights_read")
        s_tr = sem("setup_transposes")
        s_ranges = sem("ranges_ready")
        s_steps = sems("vector_steps", range(1, 5))
        s_later = sems("vector_steps_after_products", range(1, 4))
        s_xn = sems("x_normalised", range(5))
        s_xtp = sems("x_transposed", range(4))
        s_xts = sems("x_transposed_in_sbuf", range(4))
        s_prod = sems("products", range(4))
        s_tprod = sems("table_products", (0, 1, 3))
        s_prod_read = sems("products_read", range(4))
        s_tab = sems("table_rows_ready", (1, 2, 3))
        s_tabout = sems("table_stored", range(1, 5))
        s_tabfree = sems("table_rows_free", (1, 2, 3))
        s_mprod = sems("sums_transposed_or_multiplied", (1, 2))
        s_mread = sems("sums_made_of_are_read", (1, 2))
        s_nodes = sem("late_node_phases_done")
        s_passed = sem("edge_passes_done")
        s_var = sems("variances", range(1, 5))
        s_root = sems("roots", range(1, 5))
        s_scores = sem("scores_ready")
        s_exp = sem("scores_exped")
        s_relread = sem("relation_products_read")
        s_slot = [sem(f"table_slot_stored_{j}") for j in range(CH)]
        s_zeroed = sem("counts_zeroed")
        s_copied = sems("sums_copied", (1, 2))
        s_free = sems("row_slots_free", range(4))
        s_iready = sems("slot_indices", range(4))
        s_rows = [sems(f"rows_in_{l}", range(SLOTS)) for l in range(4)]
        s_hot = sems("onehots", range(4))
        s_visit = sems("visits", range(4))
        s_added = sems("sums_added", range(4))
        s_eas = [sem(f"edge_features_in_{b}") for b in range(SLOTS)]
        s_etp = sem("edge_features_transposed")
        s_ets = sem("edge_features_transposed_in_sbuf")
        s_q = sem("edge_products")
        s_h = sem("messages_steps")
        s_par = sems("slot_keys", (0, 1))
        s_xhot = sems("extra_onehots", (0, 1))
        s_xkeys = sems("extra_keys", (0, 1))
        s_xvisit = sems("extra_visits", (0, 1))
        s_xadded = sems("extra_sums_added", (0, 1))
        s_total = sem("counts_summed")
        s_total_in = sem("totals_by_partition")
        s_total_out = sem("total_of_counts")
        s_flag = sem("flag_ready")
        s_split = sem("chunks_split")
        s_first = sem("first_parts_copied")
        s_split_steps = sem("split_steps")
        s_cbf = sems("counts_converted", (2, 3))
        s_pcbf = sems("counts_converted_by_pool", (2, 3))
        s_dense = sems("dense_products", (2, 3))
        s_dread = sems("dense_products_read", (2, 3))
        s_dsum = sems("dense_sums", (2, 3))
        s_pass = {e: sem(f"passed_{e}") for e in ("act", "pool", "dve")}

        def hold(eng, name, s, v):
            eng.wait_ge(s, v)
            eng.sem_inc(s_pass[name])

        def load_range(eng, g):
            return (eng.value_load(ranges[0:1, 0, bass.ds(g, 1)], min_val=0, max_val=NW - 1),
                    eng.value_load(ranges[0:1, 1, bass.ds(g, 1)], min_val=1, max_val=NW))

        def load_packed(eng, g):
            return eng.value_load(ranges[0:1, 2, bass.ds(g, 1)], min_val=PACK, max_val=VISITS * PACK - 1)

        def load_flag(eng):
            return eng.value_load(flag[0:1, 0:1], min_val=0, max_val=1)

        def within(column):
            return nc.s_assert_within(column, 0, N - 1,
                                      skip_runtime_bounds_check_because="a window starts at a node")

        block = ctx.enter_context(nc.Block())

        def edge_loads(sp):
            def load(b, start, parts):
                sp.dma_start(eas[0:parts, b, :],
                             ea[bass.ds(start, parts * T), :].rearrange("(p k) r -> p (k r)", k=T)
                             ).then_inc(s_eas[b], 16)

            with sp.Fori(0, NI - 1) as i:
                for b in range(SLOTS):
                    sp.wait_ge(s_free[1], i * SLOTS + (b + 1))
                    load(b, i * (SLOTS * GE) + b * GE, P)
            for b in range(SLOTS):
                sp.wait_ge(s_free[1], (NI - 1) * SLOTS + b + 1)
                load(b, ((NI - 1) * SLOTS + b) * GE, P if b < SLOTS - 1 else LASTE // T)

        @block.sync
        def _(sp):
            sp.dma_start(x[:, :, :], x_in.rearrange("(w p) f -> p w f", p=WIN)).then_inc(s_x_in, 16)
            sp.wait_ge(s_padded, 1)
            for a, t in enumerate((dst, src, etype)):
                sp.dma_start(stage[:, a, 0, :], t[0:HG * GE].rearrange("(g e) -> g e", e=GE)).then_inc(s_idx_in, 16)
                sp.dma_start(stage[0:HG - 1, a, 1, :],
                             t[HG * GE:(NG - 1) * GE].rearrange("(g e) -> g e", e=GE)).then_inc(s_idx_in, 16)
                sp.dma_start(stage[HG - 1:HG, a, 1, 0:LASTE],
                             t[(NG - 1) * GE:E].rearrange("(a e) -> a e", a=1)).then_inc(s_idx_in, 16)
            sp.dma_start(w0[:, :, :], W0.rearrange("r i o -> i r o")).then_inc(s_w_in, 16)
            sp.dma_start(wself[:, :], Wself).then_inc(s_w_in, 16)
            sp.dma_start(w1raw[:, :], W1).then_inc(s_w_in, 16)
            sp.dma_start(w2raw[:, :], W2).then_inc(s_w_in, 16)
            sp.dma_start(wgraw[:, :], Wg).then_inc(s_w_in, 16)
            sp.dma_start(w3[:, :, :], W3.rearrange("(a i) o -> i a o", a=2)).then_inc(s_w_in, 16)
            sp.dma_start(att_row[:, :, :, :].rearrange("p h a d -> p (h a d)"),
                         att.rearrange("h d -> (h d)").partition_broadcast(P)).then_inc(s_w_in, 16)
            sp.dma_start(b0col[:, :], b0.rearrange("(p a) -> p a", a=1)).then_inc(s_w_in, 16)
            for n, b in enumerate((b2, bg, b3)):
                sp.dma_start(bias[:, n, :], b.partition_broadcast(P)).then_inc(s_w_in, 16)

            for j in range(CH):
                sp.sem_inc(s_slot[j], 16)
            with sp.Fori(0, NC) as c:
                for j in range(CH):
                    sp.wait_ge(s_relread, c * CH + (j + 3))
                    sp.dma_start(tables[0].ap().rearrange("(r n) f -> n r f", r=RELS)
                                 [bass.ds(c * (CH * WIN) + j * WIN, WIN), :, :],
                                 table0[:, j, :].rearrange("p (r f) -> p r f", r=RELS)).then_inc(s_slot[j], 16)

            for n in range(1, 4):
                sp.sem_inc(s_tabfree[n])
                with sp.Fori(0, NC) as c:
                    sp.wait_ge(s_tab[n], c + 1)
                    sp.dma_start(tables[n].ap()[bass.ds(c * (CH * WIN), CH * WIN), :]
                                 .rearrange("(j p) f -> p j f", p=WIN),
                                 tabs[:, :, 0:TABW[n]]).then_inc(s_tabout[n], 16)
                    sp.wait_ge(s_tabout[n], c * 16 + 16)
                    sp.sem_inc(s_tabfree[n])
                if n == 1:
                    edge_loads(sp)
            with sp.Fori(0, NC) as c:
                sp.wait_ge(s_xn[4], c + 1)
                sp.dma_start(out[bass.ds(c * (CH * WIN), CH * WIN), :].rearrange("(j p) f -> p j f", p=WIN),
                             x[:, bass.ds(c * CH, CH), :]).then_inc(s_tabout[4], 16)
            sp.wait_ge(s_tabout[4], 16 * NC)

        @block.gpsimd
        def _(pool):
            pool.memset(ident[:, :], 0.0).then_inc(s_const, 1)
            pool.wait_ge(s_const, 1)
            pool.affine_select(out=ident[:, :], in_=ident[:, :], compare_op=ALU.not_equal, fill=1.0,
                               base=0, pattern=[[-1, P]], channel_multiplier=1).then_inc(s_const, 1)
            pool.iota(iota[:, :], pattern=[[1, WIN]], base=0, channel_multiplier=0,
                      allow_small_or_imprecise_dtypes=True).then_inc(s_const, 1)
            pool.iota(wstart[:, :], pattern=[[WIN, NW]], base=0, channel_multiplier=0,
                      allow_small_or_imprecise_dtypes=True).then_inc(s_const, 1)
            pool.iota(iota16[:, :], pattern=[[1, KEYS + 1]], base=0, channel_multiplier=0,
                      allow_small_or_imprecise_dtypes=True).then_inc(s_const, 1)
            pool.iota(kcode[:, :], pattern=[[-FAR, VISITS]], base=0, channel_multiplier=0,
                      allow_small_or_imprecise_dtypes=True).then_inc(s_const, 1)
            pool.iota(kloc[:, :], pattern=[[-VW, VISITS]], base=0, channel_multiplier=0,
                      allow_small_or_imprecise_dtypes=True).then_inc(s_const, 1)
            pool.memset(ones[:, :], 1.0).then_inc(s_const, 1)
            pool.memset(eps[:, :], EPS).then_inc(s_const, 1)
            pool.wait_ge(s_x_in, 16)
            with pool.Fori(0, NC) as c:
                hold(pool, "pool", s_xtp[0], c + 1)
                pool.tensor_copy(xn[:, :, :], x[:, bass.ds(c * CH, CH), :]).then_inc(s_xn[0], 1)
            pool.wait_ge(s_ranges, 2)
            pool.memset(counts[:, LATE:NI * AB].bitcast(I32), 0).then_inc(s_zeroed, 1)

            def gathers(l):
                with pool.Fori(0, NI) as i:
                    for b in range(SLOTS):
                        hold(pool, "pool", s_iready[l], i * SLOTS + (b + 1))
                        for k in range(T):
                            pool.indirect_dma_start(
                                rows[:, b, k, 0:TABW[l]], None, tables[l].ap(),
                                bass.IndirectOffsetOnAxis(ap=idx[:, b, k:k + 1], axis=0),
                            ).then_inc(s_rows[l][b], 16)

            def counts_to_bf16(l):
                if l == 3:
                    pool.wait_ge(s_dense[2], NW + 3)
                with pool.Fori(0, NC) as c:
                    for j in POOLS:
                        hold(pool, "pool", s_dense[l], c * CH + FREED[j])
                        pool.tensor_copy(cbf[cbf_slot[j]], cnt[:, :, bass.ds(c * (CH * WIN) + j * WIN, WIN)]
                                         ).then_inc(s_pcbf[l], 1)

            for j in range(CH):
                pool.wait_ge(s_slot[j], 16 * (NC + 1))
            gathers(0)
            pool.wait_ge(s_copied[1], NC)
            pool.memset(accT[0:HID + 1, :], 0.0).then_inc(s_zeroed, 1)
            pool.wait_ge(s_tabout[1], 16 * NC)
            gathers(1)
            steps = 4
            pool.sem_inc(s_split)
            with pool.Fori(0, NC) as c:
                done = [0]

                def step(ins):
                    done[0] += 1
                    ins.then_inc(s_split_steps, 1)
                    hold(pool, "pool", s_split_steps, c * steps + done[0])

                hold(pool, "pool", s_first, c * 2 + 2)
                wd = TABW[2]
                part = [parts[2][:, bass.ds(c * CH, CH), m * wd:(m + 1) * wd] for m in range(3)]
                step(pool.tensor_tensor(left[:, :, :], tabs[:, :, 0:wd], part[0], ALU.subtract))
                step(pool.tensor_copy(part[1], left[:, :, :]))
                step(pool.tensor_tensor(left[:, :, :], left[:, :, :], part[1], ALU.subtract))
                step(pool.tensor_copy(part[2], left[:, :, :]))
                assert done[0] == steps
                pool.sem_inc(s_split)
            for l in (2, 3):
                pool.wait_ge(s_tabout[l], 16 * NC)
                if l == 2:
                    pool.wait_ge(s_flag, 1)
                pool.wait_ge(s_nodes, l - 1)
                lost = load_flag(pool)
                with pool.If(lost < 1):
                    counts_to_bf16(l)
                with pool.If(lost > 0):
                    gathers(l)

        @block.scalar
        def _(act):
            def to_sbuf(to, frm):
                return act.activation(to, frm, ACT.Copy)

            def transposed_x(n, c):
                act.wait_ge(s_xtp[n], c + 2)
                act.wait_ge(s_prod[n], c + 1)
                to_sbuf(xT[:, :, 0:WIN], flat(p0).rearrange("p (j n) -> p j n", n=P)[:, 0:CH, 0:WIN]
                        ).then_inc(s_xts[n], 1)

            def slot_indices(l, g, b):
                hold(act, "act", s_free[l], g + 1)
                to_sbuf(idx[:, b, :], (keyT if l == 0 else srcT)[:, bass.ds(g, 1), :]
                        .rearrange("p a k -> p (a k)")).then_inc(s_iready[l], 1)

            def edge_pass(l):
                if l == 1:
                    act.wait_ge(s_passed, 1)
                    act.sem_inc(s_total)
                with act.Fori(0, NI) as i:
                    for b in range(SLOTS):
                        g = i * SLOTS + b
                        slot_indices(l, g, b)
                        to_sbuf(parg[:, b, :, :], par[:, bass.ds(g, 1), :, :].rearrange("p a c k -> p (a c) k")
                                ).then_inc(s_par[l], 1)
                        if l == 1:
                            act.wait_ge(s_etp, g + 1)
                            to_sbuf(eaT[:, b % 2, :], p0[:, b % 2, 0:P]).then_inc(s_ets, 1)
                    if l == 1:
                        hold(act, "act", s_total, i + 1)
                        counted = counts[0:SB, bass.ds(i * AB, AB)]
                        act.activation(counted, counted, ACT.Copy,
                                       accum_out=total[0:SB, bass.ds(i, 1)]).then_inc(s_total, 1)

            def slow_pass(l):
                with act.Fori(0, NI) as i:
                    for b in range(SLOTS):
                        slot_indices(l, i * SLOTS + b, b)

            def warm(function):
                act.activation(warmed[:, :], ones[0:1, 0:1], function).then_inc(s_warm, 1)
                warms[0] += 1
                act.wait_ge(s_warm, warms[0])

            warms = [0]
            act.wait_ge(s_const, 9)
            warm(ACT.Copy)
            act.wait_ge(s_w_in, 16 * 11)
            act.sem_inc(s_prod[0])
            act.sem_inc(s_prod_read[0])
            act.sem_inc(s_relread, 2)
            with act.Fori(0, NC) as c:
                transposed_x(0, c)
                for j in range(CH):
                    act.wait_ge(s_tprod[0], c * CH + (j + 1))
                    act.wait_ge(s_slot[j], c * 16 + 16)
                    to_sbuf(table0[:, j, :], flat((p1, p2)[j % 2])[0:WIN, :]).then_inc(s_relread, 1)
                hold(act, "act", s_prod[0], c + 2)
                act.activation(accT[:, bass.ds(c * (CH * WIN), CH * WIN)].rearrange("p (j n) -> p j n", j=CH),
                               flat(p3).rearrange("p (j n) -> p j n", n=P)[:, 0:CH, 0:WIN],
                               ACT.Identity, bias=b0col[:, 0:1]).then_inc(s_prod_read[0], 1)
            act.wait_ge(s_ranges, 2)
            edge_pass(0)
            def counts_to_bf16(l, c, j):
                hold(act, "act", s_dense[l], c * CH + FREED[j])
                to_sbuf(cbf[cbf_slot[j]], cnt[:, :, bass.ds(c * (CH * WIN) + j * WIN, WIN)]).then_inc(s_cbf[l], 1)

            def copy_sums(n, c):
                hold(act, "act", s_mprod[n], c + 1)
                rws = (P, HID + 1)[n - 1]
                act.activation(sT[0:rws, :, 0:WIN],
                               accT[0:rws, bass.ds(c * (CH * WIN), CH * WIN)].rearrange("p (j n) -> p j n", j=CH),
                               (ACT.Relu, ACT.Copy)[n - 1]).then_inc(s_copied[n], 1)

            def projected_rows(c):
                hold(act, "act", s_prod[2], c + 2)
                to_sbuf(own[:, :, :], flat(p3)[0:WIN, 0:CH * F].rearrange("p (j f) -> p j f", j=CH)
                        ).then_inc(s_prod_read[2], 1)

            def exponentials(c):
                act.wait_ge(s_scores, c + 1)
                act.activation(small[:, 6, :], small[:, 4, :], ACT.Exp).then_inc(s_exp, 1)
                act.activation(small[:, 7, :], small[:, 5, :], ACT.Exp, scale=-1.0).then_inc(s_exp, 1)
                hold(act, "act", s_tab[2], c + 1)
                for to in (parts[2][:, bass.ds(c * CH, CH), 0:TABW[2]], acc[:, bass.ds(c * CH, CH), 0:TABW[2]]):
                    to_sbuf(to, tabs[:, :, :]).then_inc(s_first, 1)

            def node_chunk(n, c, between=(), more=False):
                if more:
                    copy_sums(n, c + 1)
                for j in between[0:4 if n < 4 else 2]:
                    counts_to_bf16(n - 1, c + 1, j)
                roots = 2 if n == 4 else 1
                if n == 4:
                    act.wait_ge(s_var[n], c * 2 + 1)
                    act.activation(small[:, 5, 0:CH], small[:, 4, 0:CH], ACT.Sqrt).then_inc(s_root[n], 1)
                    for j in between[2:4]:
                        counts_to_bf16(n - 1, c + 1, j)
                act.wait_ge(s_var[n], c * roots + roots)
                act.activation(small[:, 5, 0:CH], small[:, 0, 0:CH], ACT.Sqrt, scale=1.0 / F, bias=eps[:, 0:1]).then_inc(s_root[n], 1)
                if n < 4:
                    transposed_x(n, c)
                if n in (1, 3):
                    act.wait_ge(s_tprod[n], c + 1)
                    act.wait_ge(s_tabfree[n], c + 1)
                    frm = flat(p1)[0:WIN, 0:CH * TABW[n]].rearrange("p (j f) -> p j f", j=CH)
                    to_sbuf(tabs[:, :, 0:TABW[n]], frm).then_inc(s_tab[n], 1)

            for n in range(1, 5):
                if n < 4:
                    act.sem_inc(s_prod[n])
                if n < 3:
                    act.wait_ge(s_passed, n)
                    if n == 1:
                        warm(ACT.Sqrt)
                    copy_sums(n, 0)
                    if n == 1:
                        with act.Fori(0, NC - 1) as c:
                            node_chunk(n, c, more=True)
                        node_chunk(n, NC - 1)
                    else:
                        node_chunk(n, 0, more=True)
                        projected_rows(0)
                        with act.Fori(0, NC - 2) as c:
                            node_chunk(n, c + 1, more=True)
                            exponentials(c)
                            projected_rows(c + 1)
                        node_chunk(n, NC - 1)
                        exponentials(NC - 2)
                        projected_rows(NC - 1)
                        exponentials(NC - 1)
                if n == 1:
                    edge_pass(1)
                if n > 2:
                    if n == 3:
                        act.wait_ge(s_flag, 1)
                        act.wait_ge(s_passed, 2)
                        act.wait_ge(s_par[1], NG)
                    lost = load_flag(act)
                    with act.If(lost < 1):
                        warm(ACT.Sqrt)
                        for j in ACTS:
                            counts_to_bf16(n - 1, 0, j)
                        with act.Fori(0, NC - 1) as c:
                            node_chunk(n, c, ACTS)
                        node_chunk(n, NC - 1)
                    with act.If(lost > 0):
                        slow_pass(n - 1)
                        with act.Fori(0, NC) as c:
                            node_chunk(n, c)

        @block.tensor
        def _(pe):
            def transpose_x(n, c):
                pe.wait_ge(s_xn[n], c + 1)
                pe.wait_ge(s_xts[n], c + 1)
                for j in range(CH):
                    last = pe.transpose(win(p0, j)[:, 0:WIN], xn[:, j, :], ident[0:WIN, 0:WIN])
                last.then_inc(s_xtp[n], 1)

            def transpose_edges(i, b):
                pe.wait_ge(s_eas[b], i * 16 + 16)
                pe.transpose(p0[:, b % 2, 0:P], eas[:, b, :], ident[:, :]).then_inc(s_etp, 1)
                pe.wait_ge(s_ets, i * SLOTS + (b + 1))
                pe.matmul(p1[:, b % 2, 0:T * HID], eaT[:, b % 2, :],
                          w1b[:, :, :].rearrange("p k h -> p (k h)"), start=True, stop=True).then_inc(s_q, 1)

            def edge_pass(l):
                extra = pe.alloc_register(f"pe_extra_onehots_{l}")
                pe.reg_mov(extra, 0)
                hots, sets = ((HOTS, SETS), (1, 1))[l]

                def count_pairs(par):
                    for k in range(T):
                        pe.matmul(p0[0:SB, par, 0:KEYS - SB], lohot[:, par, k, 0:SB],
                                  keyhot[:, par, k, 0:KEYS - SB], start=(k == 0), stop=(k == T - 1))
                        pe.matmul(p1[0:SB, par, 0:SB], lohot[:, par, k, 0:SB],
                                  keyhot[:, par, k, KEYS - SB:KEYS], start=(k == 0), stop=(k == T - 1))

                def add_rows(b, par):
                    wide = (F, HID + 1)[l]
                    for k in range(T):
                        what = hbuf[:, par, k, :] if l == 1 else rows[:, b, k, 0:F]
                        last = pe.matmul(p2[0:wide, par, 0:VW], what, hot[:, par, k, :],
                                         start=(k == 0), stop=(k == T - 1))
                    return last

                def group(i, b):
                    g, par = i * SLOTS + b, b % 2
                    visits = load_packed(pe, g) // PACK
                    pe.wait_ge(s_hot[l], i * (hots * SLOTS) + hots * (b + 1))
                    pe.wait_ge(s_added[l], i * (sets * SLOTS) + sets * (b + 1))
                    if l == 0:
                        count_pairs(par)
                        pe.wait_ge(s_rows[l][b], i * (16 * T) + 16 * T)
                    else:
                        pe.wait_ge(s_h, i * (2 * SLOTS) + 2 * (b + 1))
                    add_rows(b, par).then_inc(s_visit[l], 1)
                    with pe.If(visits > 1):
                        with pe.Fori(1, visits):
                            pe.reg_add(extra, extra, XHOTS[l])
                            pe.wait_ge(s_xhot[l], pe.snap(extra))
                            if l == 0:
                                count_pairs(par)
                            add_rows(b, par).then_inc(s_xvisit[l], 1)

                if l == 1:
                    transpose_edges(0, 0)
                with pe.Fori(0, NI - 1) as i:
                    for b in range(SLOTS):
                        if l == 1:
                            transpose_edges(*((i, b + 1) if b < SLOTS - 1 else (i + 1, 0)))
                        group(i, b)
                for b in range(SLOTS):
                    if l == 1 and b < SLOTS - 1:
                        transpose_edges(NI - 1, b + 1)
                    group(NI - 1, b)

            def slow_pass(l):
                visits = pe.alloc_register(f"pe_visits_{l}")
                pe.reg_mov(visits, 0)
                wide = SUMW[l]
                with pe.Fori(0, NI) as i:
                    for b in range(SLOTS):
                        pe.wait_ge(s_rows[l][b], i * (16 * T) + 16 * T)
                        lo, hi = load_range(pe, i * SLOTS + b)
                        with pe.Fori(lo, hi):
                            pe.reg_add(visits, visits, 1)
                            v = pe.snap(visits)
                            pe.wait_ge(s_hot[l], v)
                            pe.wait_ge(s_added[l], v)
                            for k in range(T):
                                last = pe.matmul(p2[0:WIN, 0, 0:wide], onehot[:, k, :], rows[:, b, k, 0:wide],
                                                 start=(k == 0), stop=(k == T - 1))
                            last.then_inc(s_visit[l], 1)

            def dense_window(l, c, j):
                wide = 3 * TABW[l]
                if j in POOLS:
                    pe.wait_ge(s_pcbf[l], c * len(POOLS) + (POOLS.index(j) + 1))
                else:
                    pe.wait_ge(s_cbf[l], c * len(ACTS) + (ACTS.index(j) + 1))
                pe.wait_ge(s_dread[l], c * CH + READ[j])
                for h in range(VW):
                    last = pe.matmul(dense_bank[j][:, 0:wide], cbf[cbf_slot[j]][:, h, :],
                                     parts[l][:, h, 0:wide], start=(h == 0), stop=(h == VW - 1))
                last.then_inc(s_dense[l], 1)

            pe.wait_ge(s_const, 2)
            pe.wait_ge(s_w_in, 16 * 11)
            pe.transpose(win(p3, 0)[:, 0:HID], w1raw[:, 0:F], ident[0:HID, 0:HID])
            pe.transpose(win(p3, 2), w2raw[:, 0:F], ident[:, :])
            pe.transpose(win(p3, 3)[0:HID, :], w2raw[:, F:F + HID], ident[:, :])
            pe.wait_ge(s_rep, 1)
            pe.transpose(win(p3, 1)[:, 0:HID], w1rep[:, :, :].rearrange("h k r -> h (k r)"), ident[0:HID, 0:HID])
            pe.transpose(win(p3, 4), wgraw[:, :], ident[:, :]).then_inc(s_tr, 1)
            pe.wait_ge(s_cast, 3)
            for a in range(3):
                for h in range(2):
                    for k in range(T):
                        last = pe.transpose((p0, p1, p2)[a][:, h, k * HG:(k + 1) * HG],
                                            staged[:, a, h, :].rearrange("g (e k) -> g k e", k=T)[:, k, :],
                                            ident[0:HG, 0:HG])
            pe.wait_ge(s_reach, 1)
            for r in range(3):
                for h in range(2):
                    pe.transpose((p0, p1, p2)[r][0:1, h, T * HG:(T + 1) * HG], reach[:, r, h:h + 1],
                                 ident[0:HG, 0:HG])
            pe.wait_ge(s_diag, 1)
            pe.wait_ge(s_w1_read, 1)
            for h in range(2):
                last = pe.matmul(p3[:, h, 0:HG], ones[0:HG, :], diag[:, h, :], start=True, stop=True)
            last.then_inc(s_tr, 1)
            pe.wait_ge(s_ranges, 1)

            pe.sem_inc(s_xts[0])
            pe.sem_inc(s_xtp[0])
            with pe.Fori(0, NC) as c:
                transpose_x(0, c)
                pe.wait_ge(s_xts[0], c + 2)
                pe.wait_ge(s_prod_read[0], c + 1)
                for j in range(CH):
                    pe.wait_ge(s_relread, c * CH + READ[j])
                    for h in range(2):
                        last = pe.matmul((p1, p2)[j % 2][0:WIN, h, :], xT[:, j, 0:WIN],
                                         w0[:, 4 * h:4 * h + 4, :].rearrange("p r f -> p (r f)"),
                                         start=True, stop=True)
                    last.then_inc(s_tprod[0], 1)
                for j in range(CH):
                    last = pe.matmul(win(p3, j)[:, 0:WIN], wself[:, :], xT[:, j, 0:WIN], start=True, stop=True)
                last.then_inc(s_prod[0], 1)
            edge_pass(0)

            def use_sums(n, c):
                pe.wait_ge(s_copied[n], c + 1)
                pe.wait_ge(s_mread[n], c + 1)
                if n == 1:
                    for j in range(CH):
                        last = pe.transpose(win(p2, j)[0:WIN, :], sT[:, j, 0:WIN], ident[:, :])
                    last.then_inc(s_mprod[n], 1)
                if n == 2:
                    for j in range(CH):
                        pe.matmul(win(p2, j)[0:WIN, :], sT[0:HID, j, 0:WIN], w2b[:, :], start=True, stop=True)
                    for j in range(CH):
                        last = pe.matmul(p1[0:WIN, 1, j:j + 1], sT[0:HID + 1, j, 0:WIN],
                                         ident[0:HID + 1, HID:HID + 1], start=True, stop=True)
                    last.then_inc(s_mprod[n], 1)

            def node_chunk(n, c, between=(), more=False):
                if more:
                    use_sums(n, c + 1)
                for j in between[0:3]:
                    dense_window(n - 1, c + 1, j)
                transpose_x(n, c)
                for j in between[3:4]:
                    dense_window(n - 1, c + 1, j)
                pe.wait_ge(s_xts[n], c + 2)
                pe.wait_ge(s_prod_read[n], c + 1)
                if n in (1, 3):
                    wide, w_tab = TABW[n], (w1a[:, :] if n == 1 else w3[:, 1, :])
                    if n == 1:
                        outs = [p1[0:WIN, 0, j * wide:(j + 1) * wide] for j in range(CH)]
                    else:
                        outs = [win(p1, j)[0:WIN, :] for j in range(CH)]
                    pe.wait_ge(s_tabfree[n], c + 1)
                    for j in range(CH):
                        last = pe.matmul(outs[j], xT[:, j, 0:WIN], w_tab, start=True, stop=True)
                    last.then_inc(s_tprod[n], 1)
                w_own = (None, w2a[:, :], wg[:, :], w3[:, 0, :])[n]
                for j in range(CH):
                    last = pe.matmul(win(p3, j)[0:WIN, :], xT[:, j, 0:WIN], w_own, start=True, stop=True)
                last.then_inc(s_prod[n], 1)
                for j in between[4:5]:
                    dense_window(n - 1, c + 1, j)

            for n in range(1, 5):
                if n < 4:
                    pe.sem_inc(s_xts[n])
                    pe.sem_inc(s_xtp[n])
                if n == 2:
                    pe.wait_ge(s_total_in, 1)
                    pe.matmul(p3[0:1, 0, 0:1], totals[0:SB, 0:1], ones[0:SB, 0:1], start=True, stop=True
                              ).then_inc(s_total_out, 1)
                if n < 3:
                    pe.sem_inc(s_mprod[n])
                    use_sums(n, 0)
                    with pe.Fori(0, NC - 1) as c:
                        node_chunk(n, c, more=True)
                    node_chunk(n, NC - 1)
                if n == 1:
                    edge_pass(1)
                if n > 2:
                    pe.wait_ge(s_nodes, n - 2)
                    lost = load_flag(pe)
                    with pe.If(lost < 1):
                        pe.sem_inc(s_dense[n - 1], 3)
                        for j in range(CH):
                            dense_window(n - 1, 0, j)
                        with pe.Fori(0, NC - 1) as c:
                            if n == 3:
                                node_chunk(n, c, range(CH))
                            else:
                                for j in range(CH):
                                    dense_window(n - 1, c + 1, j)
                        if n == 3:
                            node_chunk(n, NC - 1)
                    with pe.If(lost > 0):
                        slow_pass(n - 1)
                        if n == 3:
                            with pe.Fori(0, NC) as c:
                                node_chunk(n, c)

        @block.vector
        def _(dve):
            done = [0]

            def setup(ins):
                done[0] += 1
                ins.then_inc(s_set, 1)
                dve.wait_ge(s_set, done[0])

            setup(dve.memset(stage[:, 0, 1, :], NPAD))
            setup(dve.memset(stage[:, 1:3, 1, :], 0))
            dve.sem_inc(s_padded)
            setup(dve.memset(w1b[:, :, :], 0.0))
            dve.wait_ge(s_w_in, 16 * 11)
            for k in range(T):
                setup(dve.tensor_copy(w1rep[:, k, :], w1raw[:, F:F + R]))
            dve.sem_inc(s_rep)
            dve.wait_ge(s_idx_in, 16 * 9)
            setup(dve.tensor_copy(staged[:, 0:2, :, :], stage[:, 0:2, :, :]))
            setup(dve.scalar_tensor_tensor(staged[:, 2, :, :], stage[:, 2, :, :], float(N), stage[:, 1, :, :],
                                           ALU.mult, ALU.add))
            dve.sem_inc(s_cast, 3)
            dve.wait_ge(s_const, 8)

            def floor_div(to, frm, raw, by):
                setup(dve.tensor_scalar(raw, frm, -(by - 1) / 2, 1.0 / by, ALU.add, ALU.mult))
                setup(dve.tensor_scalar(raw, raw, 12582912.0, None, ALU.add))
                setup(dve.tensor_scalar(to, raw, -12582912.0, None, ALU.add))

            setup(dve.tensor_reduce(ext[:, :, 0], staged[:, 0, :, :], X, ALU.min))
            setup(dve.tensor_reduce(ext[:, :, 1], staged[:, 0, :, :], X, ALU.max))
            setup(dve.tensor_scalar(ext[:, :, 1], ext[:, :, 1], N - 1.0, None, ALU.min))
            for h in range(2):
                setup(dve.tensor_scalar(diag[:, h, :], ident[0:HG, 0:HG], ext[:, h, 0:1], None, ALU.mult))
            dve.sem_inc(s_diag)
            floor_div(reach[:, 0, :], ext[:, :, 0], ext[:, :, 2], WIN)
            floor_div(reach[:, 1, :], ext[:, :, 1], ext[:, :, 2], WIN)
            setup(dve.tensor_scalar(reach[:, 1, :], reach[:, 1, :], 1.0, None, ALU.add))
            setup(dve.tensor_tensor(ext[:, :, 3], ext[:, :, 1], ext[:, :, 0], ALU.subtract))
            floor_div(ext[:, :, 3], ext[:, :, 3], ext[:, :, 2], VW)
            setup(dve.tensor_scalar(ext[:, :, 3], ext[:, :, 3], 1.0, float(PACK), ALU.add, ALU.mult))
            setup(dve.tensor_tensor(reach[:, 2, :], ext[:, :, 3], ext[:, :, 0], ALU.add))
            dve.sem_inc(s_reach)
            dve.wait_ge(s_tr, 1)
            setup(dve.tensor_copy(w1a[:, :], win(p3, 0)[:, 0:HID]))
            for k in range(T):
                setup(dve.tensor_copy(w1b[R * k:R * k + R, k, :], win(p3, 1)[R * k:R * k + R, 0:HID]))
            setup(dve.tensor_copy(w2a[:, :], win(p3, 2)))
            setup(dve.tensor_copy(w2b[:, :], win(p3, 3)[0:HID, :]))
            setup(dve.tensor_copy(wg[:, :], win(p3, 4)))
            dve.sem_inc(s_w1_read)
            dve.wait_ge(s_tr, 2)
            for a, to in enumerate((dstT, srcT, keyT)):
                for h in range(2):
                    setup(dve.tensor_copy(to[:, h * HG:(h + 1) * HG, :].rearrange("p g k -> p k g"),
                                          (p0, p1, p2)[a][:, h, 0:T * HG].rearrange("p (k g) -> p k g", k=T)))
            for r in range(3):
                for h in range(2):
                    setup(dve.tensor_copy(ranges[0:1, r, h * HG:(h + 1) * HG],
                                          (p0, p1, p2)[r][0:1, h, T * HG:(T + 1) * HG]))
            for h in range(2):
                gs = slice(h * HG, (h + 1) * HG)
                setup(dve.tensor_tensor(setf[0][:, gs, :], dstT[:, gs, :],
                                        p3[:, h, 0:HG].unsqueeze(2).to_broadcast([P, HG, T]), ALU.subtract))
            dve.sem_inc(s_ranges)
            setup(dve.tensor_copy(par[:, :, 2, :], setf[0]))
            setup(dve.tensor_copy(setf[1], srcT[:, :, :]))
            floor_div(setf[2], setf[1], setf[3], SB)
            setup(dve.scalar_tensor_tensor(par[:, :, 1, :], setf[2], -float(SB), setf[1], ALU.mult, ALU.add))
            setup(dve.scalar_tensor_tensor(setf[1], setf[2], float(VW), setf[0], ALU.mult, ALU.add))
            floor_div(setf[2], setf[0], setf[3], VW)
            setup(dve.scalar_tensor_tensor(par[:, :, 0, :], setf[2], float(FAR - VW), setf[1], ALU.mult, ALU.add))
            setup(dve.memset(accT[:, N:NPAD], 0.0))
            dve.sem_inc(s_ranges)

            def wide(t):
                return flat(t)[0:WIN, 0:CH * F].rearrange("p (j f) -> p j f", j=CH)

            def biased(n):
                return bias[0:WIN, n:n + 1, :].to_broadcast([WIN, CH, F])

            def by_head(t):
                return t.rearrange("p j (h d) -> p j h d", h=HEADS)

            def col(n):
                return small[:, n, 0:CH]

            def each(n):
                return col(n).unsqueeze(2).to_broadcast([WIN, CH, F])

            def start_nodes(n):
                if n < 4:
                    dve.sem_inc(s_prod_read[n])
                if n in (1, 2):
                    dve.sem_inc(s_mread[n])

            def steps_of(n, part, c, between, taken):
                done = (s_steps, s_later)[part][n]

                def step(ins):
                    taken[0] += 1
                    ins.then_inc(done, 1)
                    dve.wait_ge(done, c * STEPS[n][part] + taken[0])
                    if between and taken[0] in ADDS_AFTER[n][part]:
                        between((0, len(ADDS_AFTER[n][0]))[part] + ADDS_AFTER[n][part].index(taken[0]))

                return step

            def node_chunk(n, c, between=None):
                normalise(n, c, between)
                if n < 4:
                    use_products(n, c, between)

            def normalise(n, c, between=None):
                taken = [0]
                step = steps_of(n, 0, c, between, taken)
                roots = 2 if n == 4 else 1
                xc = x[:, bass.ds(c * CH, CH), :]
                ac = acc[:, bass.ds(c * CH, CH), :]
                bc = base[:, bass.ds(c * CH, CH), :]
                if n == 1:
                    dve.wait_ge(s_mprod[n], c + 2)
                    step(dve.tensor_tensor(ta[:, :, :], wide(p2), xc, ALU.add))
                    dve.sem_inc(s_mread[n])
                if n == 2:
                    dve.wait_ge(s_mprod[n], c + 2)
                    step(dve.tensor_scalar(col(0), p1[0:WIN, 1, 0:CH], 1.0, None, ALU.max))
                    step(dve.reciprocal(col(1), col(0)))
                    step(dve.tensor_tensor(tb[:, :, :], wide(p2), each(1), ALU.mult))
                    dve.sem_inc(s_mread[n])
                    step(dve.tensor_tensor(tb[:, :, :], tb[:, :, :], bc, ALU.add))
                    step(dve.scalar_tensor_tensor(ta[:, :, :], tb[:, :, :], 0.01, tb[:, :, :], ALU.mult, ALU.max))
                    step(dve.tensor_tensor(ta[:, :, :], ta[:, :, :], xc, ALU.add))
                if n == 3:
                    s5 = small[:, 0, :].rearrange("p (j h) -> p j h", j=CH)
                    s6 = small[:, 1, :].rearrange("p (j h) -> p j h", j=CH)
                    step(dve.tensor_tensor(s5, ac[:, :, F:F + HEADS], ac[:, :, F + HEADS:F + 2 * HEADS], ALU.add))
                    step(dve.reciprocal(s6, s5))
                    step(dve.tensor_tensor(by_head(ta[:, :, :]), by_head(ac[:, :, 0:F]),
                                           s6.unsqueeze(3).to_broadcast([WIN, CH, HEADS, HD]), ALU.mult))
                    step(dve.tensor_tensor(ta[:, :, :], ta[:, :, :], biased(1), ALU.add))
                    step(dve.tensor_tensor(ta[:, :, :], ta[:, :, :], xc, ALU.add))
                if n == 4:
                    step(dve.tensor_scalar(ta[:, :, :], ac[:, :, 0:F], 0.0, None, ALU.max))
                    step(dve.tensor_tensor(tb[:, :, :], ta[:, :, :], ta[:, :, :], ALU.mult))
                    step(dve.tensor_reduce(col(0), tb[:, :, :], X, ALU.add))
                    step(dve.tensor_scalar(col(4), col(0), 1e-24, None, ALU.max))
                    dve.sem_inc(s_var[n])
                    dve.wait_ge(s_root[n], c * 2 + 1)
                    step(dve.reciprocal(col(1), col(5)))
                    step(dve.tensor_tensor(ta[:, :, :], ta[:, :, :], each(1), ALU.mult))
                    step(dve.tensor_tensor(ta[:, :, :], ta[:, :, :], xc, ALU.add))
                if n > 0:
                    step(dve.tensor_reduce(col(2), ta[:, :, :], X, ALU.add))
                    step(dve.scalar_tensor_tensor(ta[:, :, :], each(2), -1.0 / F, ta[:, :, :], ALU.mult, ALU.add))
                    step(dve.tensor_tensor(tb[:, :, :], ta[:, :, :], ta[:, :, :], ALU.mult))
                    step(dve.tensor_reduce(col(0), tb[:, :, :], X, ALU.add))
                    dve.sem_inc(s_var[n])
                    dve.wait_ge(s_root[n], c * roots + roots)
                    step(dve.reciprocal(col(2), col(5)))
                if n == 4:
                    dve.tensor_tensor(xc, ta[:, :, :], each(2), ALU.mult).then_inc(s_xn[4], 1)
                    step(dve.tensor_copy(col(6), col(2)))
                else:
                    dve.wait_ge(s_xtp[n], c + 1)
                    step(dve.tensor_tensor(xn[:, :, :], ta[:, :, :], each(2), ALU.mult))
                    dve.sem_inc(s_xn[n])
                    step(dve.tensor_copy(xc, xn[:, :, :]))
                assert taken[0] == STEPS[n][0], (n, 0, taken[0])

            def use_products(n, c, between=None):
                taken = [0]
                step = steps_of(n, 1, c, between, taken)
                ac = acc[:, bass.ds(c * CH, CH), :]
                bc = base[:, bass.ds(c * CH, CH), :]
                dve.wait_ge(s_prod[n], c + 2)
                if n == 1:
                    step(dve.tensor_tensor(bc, wide(p3), biased(0), ALU.add))
                    dve.sem_inc(s_prod_read[n])
                if n == 2:
                    dve.wait_ge(s_prod_read[n], c + 2)
                    step(dve.scalar_tensor_tensor(tb[:, :, :], own[:, :, :], 0.2, own[:, :, :], ALU.mult, ALU.max))
                    for a in range(2):
                        step(dve.tensor_tensor(by_head(xs[:, :, :]), by_head(tb[:, :, :]),
                                               att_row[0:WIN, :, a, :].unsqueeze(1)
                                               .to_broadcast([WIN, CH, HEADS, HD]), ALU.mult))
                        step(dve.tensor_reduce(small[:, 4 + a, :],
                                               xs[:, :, :].rearrange("p j (h d) -> p (j h) d", h=HEADS),
                                               X, ALU.add))
                    dve.sem_inc(s_scores)
                    dve.wait_ge(s_exp, c * 2 + 2)
                    dve.wait_ge(s_tabfree[n], c + 1)
                    dve.wait_ge(s_split, c + 1)
                    e = small[:, 6, :].rearrange("p (j h) -> p j h", j=CH)
                    step(dve.tensor_copy(tabs[:, :, F:F + HEADS], e))
                    step(dve.tensor_tensor(by_head(tabs[:, :, 0:F]), by_head(own[:, :, :]),
                                           e.unsqueeze(3).to_broadcast([WIN, CH, HEADS, HD]), ALU.mult))
                    dve.sem_inc(s_tab[n])
                    step(dve.tensor_scalar(ac[:, :, F + HEADS:F + 2 * HEADS],
                                           small[:, 7, :].rearrange("p (j h) -> p j h", j=CH),
                                           1e-9, None, ALU.mult))
                if n == 3:
                    step(dve.tensor_tensor(ac[:, :, 0:F], wide(p3), biased(2), ALU.add))
                    dve.sem_inc(s_prod_read[n])
                    dve.wait_ge(s_tab[n], c + 1)
                    wd = TABW[n]
                    part = [parts[n][:, bass.ds(c * CH, CH), m * wd:(m + 1) * wd] for m in range(3)]
                    step(dve.tensor_copy(part[0], tabs[:, :, 0:wd]))
                    step(dve.tensor_tensor(rest[:, :, 0:wd], tabs[:, :, 0:wd], part[0], ALU.subtract))
                    step(dve.tensor_copy(part[1], rest[:, :, 0:wd]))
                    step(dve.tensor_tensor(rest[:, :, 0:wd], rest[:, :, 0:wd], part[1], ALU.subtract))
                    step(dve.tensor_copy(part[2], rest[:, :, 0:wd]))
                assert taken[0] == STEPS[n][1], (n, 1, taken[0])

            def edge_pass(l):
                counted = {e: dve.alloc_register(f"dve_extra_{e}_{l}") for e in ("keys", "visits", "sums")}
                sets = (SETS, 1)[l]
                feats = (F, HID + 1)[l]

                def count(what, by):
                    dve.reg_add(counted[what], counted[what], by)
                    return dve.snap(counted[what])

                def onehots(par, keys, sources, places, s_built):
                    if l == 0:
                        for k in range(T):
                            dve.tensor_scalar(keyhot[:, par, k, :], iota16[:, :], keys[:, k:k + 1], None,
                                              ALU.is_equal).then_inc(s_built, 1)
                        if sources is not None:
                            for k in range(T):
                                dve.tensor_scalar(lohot[:, par, k, :], iota16[:, 0:SB + 1], sources[:, k:k + 1], None,
                                                  ALU.is_equal).then_inc(s_built, 1)
                    dve.tensor_tensor(hot[:, par, :, :], iota[:, 0:VW].unsqueeze(1).to_broadcast([P, T, VW]),
                                      places.unsqueeze(2).to_broadcast([P, T, VW]), ALU.is_equal).then_inc(s_built, 1)

                def build(i, b):
                    par = b % 2
                    dve.wait_ge(s_par[l], i * SLOTS + (b + 1))
                    onehots(par, parg[:, b, 0, :], parg[:, b, 1, :], parg[:, b, 2, :], s_hot[l])
                    if l == 1:
                        dve.wait_ge(s_rows[l][b], i * (16 * T) + 16 * T)
                        dve.wait_ge(s_q, i * SLOTS + (b + 1))
                        dve.tensor_tensor(hbuf[:, par, :, 0:HID],
                                          p1[:, par, 0:T * HID].rearrange("p (k h) -> p k h", k=T),
                                          rows[:, b, :, 0:HID], ALU.add).then_inc(s_h, 1)
                        dve.wait_ge(s_h, i * (2 * SLOTS) + (2 * b + 1))
                        dve.scalar_tensor_tensor(hbuf[:, par, :, 0:HID], hbuf[:, par, :, 0:HID], 0.01,
                                                 hbuf[:, par, :, 0:HID], ALU.mult, ALU.max).then_inc(s_h, 1)

                def add(par, first, s_done):
                    cols = accT[0:feats, bass.ds(first, VW)]
                    dve.tensor_tensor(cols, cols, p2[0:feats, par, 0:VW], ALU.add).then_inc(s_done, 1)
                    if l == 0:
                        for blocks, bank in ((slice(0, VW - CH), p0[0:SB, par, 0:KEYS - SB]),
                                             (slice(VW - CH, VW), p1[0:SB, par, 0:SB])):
                            pairs = cnt[:, blocks, bass.ds(first, VW)]
                            dve.tensor_tensor(pairs, pairs, bank.rearrange("p (h d) -> p h d", d=VW), ALU.add
                                              ).then_inc(s_done, 1)

                def group(i, b, after):
                    g, par = i * SLOTS + b, b % 2
                    packed = load_packed(dve, g)
                    first, visits = packed % PACK, packed // PACK
                    if after is not None:
                        build(*after)
                    dve.wait_ge(s_visit[l], g + 1)
                    dve.wait_ge(s_added[l], i * (sets * SLOTS) + sets * (b + 2))
                    add(par, within(first), s_added[l])
                    with dve.If(visits > 1):
                        hold(dve, "dve", s_added[l], i * (sets * SLOTS) + sets * (b + 3))
                        with dve.Fori(1, visits) as k:
                            for a, by in ((0, kcode), (2, kloc)):
                                dve.tensor_scalar(parx[:, a, :], parg[:, b, a, :], by[:, bass.ds(k, 1)], None, ALU.add
                                                  ).then_inc(s_xkeys[l], 1)
                            hold(dve, "dve", s_xkeys[l], count("keys", 2))
                            onehots(par, parx[:, 0, :], None, parx[:, 2, :], s_xhot[l])
                            hold(dve, "dve", s_xvisit[l], count("visits", 1))
                            add(par, within(first + k * VW), s_xadded[l])
                            hold(dve, "dve", s_xadded[l], count("sums", sets))
                    dve.sem_inc(s_free[l])

                for r in counted.values():
                    dve.reg_mov(r, 0)
                dve.sem_inc(s_added[l], 2 * sets)
                if l == 0:
                    for j in range(CH):
                        dve.wait_ge(s_slot[j], 16 * (NC + 1))
                    setup(dve.memset(counts[:, 0:LATE].bitcast(I32), 0))
                    dve.wait_ge(s_zeroed, 1)
                    dve.wait_ge(s_prod_read[0], NC + 1)
                else:
                    dve.wait_ge(s_tabout[1], 16 * NC)
                    setup(dve.memset(hbuf[:, :, :, HID], 1.0))
                    dve.wait_ge(s_zeroed, 2)
                dve.sem_inc(s_free[l], SLOTS)
                build(0, 0)
                with dve.Fori(0, NI - 1) as i:
                    for b in range(SLOTS):
                        group(i, b, (i, b + 1) if b < SLOTS - 1 else (i + 1, 0))
                for b in range(SLOTS):
                    group(NI - 1, b, (NI - 1, b + 1) if b < SLOTS - 1 else None)
                dve.wait_ge(s_added[l], sets * (NG + 2))
                dve.sem_inc(s_passed)

            def find_flag():
                dve.wait_ge(s_total, NI + 1)
                setup(dve.tensor_reduce(totals[0:SB, 0:1], total[0:SB, :], X, ALU.add))
                dve.sem_inc(s_total_in)
                dve.wait_ge(s_total_out, 1)
                setup(dve.tensor_scalar(flag[0:1, 0:1], p3[0:1, 0, 0:1], E - 0.5, None, ALU.is_lt))
                dve.sem_inc(s_flag)

            def slow_pass(l):
                visits = dve.alloc_register(f"dve_visits_{l}")
                wd = SUMW[l]
                dve.sem_inc(s_free[l], SLOTS)
                dve.sem_inc(s_added[l])
                dve.reg_mov(visits, 0)
                with dve.Fori(0, NI) as i:
                    for b in range(SLOTS):
                        g = i * SLOTS + b
                        lo, hi = load_range(dve, g)
                        with dve.Fori(lo, hi) as w:
                            dve.reg_add(visits, visits, 1)
                            v = dve.snap(visits)
                            dve.scalar_tensor_tensor(
                                onehot[:, :, :], iota[:, :].unsqueeze(1).to_broadcast([P, T, WIN]),
                                wstart[:, bass.ds(w, 1)],
                                dstT[:, bass.ds(g, 1), :].rearrange("p a k -> p (a k)").unsqueeze(2)
                                .to_broadcast([P, T, WIN]), ALU.add, ALU.is_equal).then_inc(s_hot[l], 1)
                            dve.wait_ge(s_visit[l], v)
                            dve.wait_ge(s_added[l], v)
                            aw = acc[:, bass.ds(w, 1), 0:wd].rearrange("p a f -> p (a f)")
                            dve.tensor_tensor(aw, aw, p2[0:WIN, 0, 0:wd], ALU.add).then_inc(s_added[l], 1)
                        dve.sem_inc(s_free[l])
                hold(dve, "dve", s_added[l], dve.snap(visits) + 1)

            def dense_add(l, c, j):
                wd = TABW[l]
                dve.wait_ge(s_dense[l], c * CH + (j + 4))
                dve.wait_ge(s_dsum[l], c * CH + (j + 1))
                dve.tensor_reduce(three[:, j % 3, 0:wd], dense_bank[j][:, 0:3 * wd].rearrange("p (m f) -> p f m", m=3),
                                  X, ALU.add).then_inc(s_dread[l], 1)
                dve.wait_ge(s_dread[l], c * CH + (j + 3))
                aw = acc[:, bass.ds(c * CH + j, 1), 0:wd].rearrange("p a f -> p (a f)")
                dve.tensor_tensor(aw, aw, three[:, j % 3, 0:wd], ALU.add).then_inc(s_dsum[l], 1)

            def dense_chunk(l, c):
                for j in range(CH):
                    dense_add(l, c, j)

            for n in range(5):
                if n > 0:
                    start_nodes(n)
                if n in (1, 2):
                    normalise(n, 0)
                    with dve.Fori(0, NC - 1) as c:
                        normalise(n, c + 1)
                        use_products(n, c)
                    use_products(n, NC - 1)
                if n in (0, 1):
                    edge_pass(n)
                if n == 1:
                    find_flag()
                if n > 2:
                    l = n - 1
                    lost = load_flag(dve)
                    with dve.If(lost < 1):
                        dve.sem_inc(s_dread[l], 2)
                        dve.sem_inc(s_dsum[l], 2)
                        dense_chunk(l, 0)
                        with dve.Fori(0, NC - 1) as c:
                            hold(dve, "dve", s_dsum[l], c * CH + (CH + 2))
                            node_chunk(n, c, lambda j: dense_add(l, c + 1, j))
                        dve.wait_ge(s_dsum[l], NW + 2)
                        node_chunk(n, NC - 1)
                    with dve.If(lost > 0):
                        slow_pass(l)
                        with dve.Fori(0, NC) as c:
                            node_chunk(n, c)
                if n in (2, 3):
                    if n == 2:
                        dve.wait_ge(s_split, NC + 1)
                    dve.sem_inc(s_nodes)


_INS = ["x", "src", "dst", "edge_attr_32", "edge_type_8", "L0_gnn_weight", "L0_gnn_self_loop_weight",
        "L0_gnn_bias", "L1_gnn_W1", "L1_gnn_W2", "L1_gnn_b2", "L2_gnn_W", "L2_gnn_att", "L2_gnn_bias",
        "L3_gnn_W", "L3_gnn_b"]


def kernel(**inputs):
    import numpy as _np
    import concourse.bacc as _bacc
    from concourse import mybir as _mybir
    from concourse.bass_utils import run_bass_kernel_spmd as _run

    nc = _bacc.Bacc("TRN2", target_bir_lowering=False, num_devices=1)
    arrays, args = {}, []
    for name in _INS:
        a = _np.ascontiguousarray(inputs[name])
        arrays[f"in_{name}"] = a
        args.append(nc.dram_tensor(f"in_{name}", a.shape, _mybir.dt.from_np(a.dtype), kind="ExternalInput").ap())
    args.append(nc.dram_tensor("out_0", (3125, 128), _mybir.dt.float32, kind="ExternalOutput").ap())
    resgnn(nc, *args)
    r = _run(nc, [arrays], core_ids=[0])
    return r.results[0]["out_0"]
```
